# Optimizing a Trainium2 kernel written in Bass

```python
import numpy as np
import jax
import jax.numpy as jnp

def _softmax(x, axis=-1):
    return jax.nn.softmax(x, axis=axis)

def _gelu(x):
    return jax.nn.gelu(x, approximate=True)

def _silu(x):
    return jax.nn.silu(x)

def _sigmoid(x):
    return jax.nn.sigmoid(x)

def _layernorm(x, axis=-1, eps=1e-05):
    m = jnp.mean(x, axis=axis, keepdims=True)
    v = jnp.var(x, axis=axis, keepdims=True)
    return (x - m) / jnp.sqrt(v + eps)

def _scatter_add(tgt, idx, src, axis=0):
    return tgt.at[idx].add(src)

def _segment_sum(src, seg, n):
    return jax.ops.segment_sum(src, seg, n)
kernel_name = 'mk_xattn_ffn_d1_seqx_r8_1d647a'

def setup_inputs(seed: int=0):
    np.random.seed(seed)
    _w = jnp.asarray

    def _rec_inputs():
        import jax
        import jax.numpy as jnp
        _rk = jax.random.key(seed)
        x = -0.0005207 + 1.001 * jax.random.normal(jax.random.fold_in(_rk, 1), (2, 512, 128), jnp.float32)
        _lenS = 512 - jax.random.randint(jax.random.fold_in(_rk, 7), (2,), 0, max(1, 512 // 4) + 1, jnp.int32)
        _lenS2 = 77 - jax.random.randint(jax.random.fold_in(_rk, 8), (2,), 0, max(1, 77 // 4) + 1, jnp.int32)
        _ctx_1024P = jax.random.normal(jax.random.fold_in(_rk, 11), (2, 16, 128), jnp.float32)
        _ctx_1024c = jax.random.dirichlet(jax.random.fold_in(_rk, 511), 0.3 * jnp.ones((16,), jnp.float32), (2, 77))
        _ctx_1024t = jnp.einsum('bsk,bkd->bsd', _ctx_1024c, _ctx_1024P)
        _ctx_1024t = _ctx_1024t * jax.lax.rsqrt(jnp.mean(jnp.square(_ctx_1024t)) + 1e-12) * 0.953939
        ctx_1024 = -0.000514642 + 1.00011 * (_ctx_1024t + 0.3 * jax.random.normal(jax.random.fold_in(_rk, 611), (2, 77, 128), jnp.float32))
        return (x, ctx_1024)
    x, ctx_1024 = _rec_inputs()

    def _L0_xattn_setup():
        import jax, jax.numpy as jnp
        import numpy as np
        EMBED_DIM = 128
        NUM_HEADS = 16
        HEAD_DIM = EMBED_DIM // NUM_HEADS
        WINDOW = 64

        def apply_rope(x):
            B, H, S, d = x.shape
            half = d // 2
            pos = jnp.arange(S, dtype=x.dtype)
            freqs = 1.0 / 10000.0 ** (jnp.arange(half, dtype=x.dtype) / half)
            ang = pos[:, None] * freqs[None, :]
            cos, sin = (jnp.cos(ang), jnp.sin(ang))
            x1, x2 = (x[..., :half], x[..., half:])
            return jnp.concatenate([x1 * cos - x2 * sin, x1 * sin + x2 * cos], axis=-1)

        def _forward(query, key, value, q_w, q_b, k_w, k_b, v_w, v_b, o_w, o_b):
            B, S_q, D = query.shape
            S_k = key.shape[1]
            H, d, W = (NUM_HEADS, HEAD_DIM, WINDOW)
            q = (query @ q_w.T + q_b).reshape(B, S_q, H, d).transpose(0, 2, 1, 3)
            k = (key @ k_w.T + k_b).reshape(B, S_k, H, d).transpose(0, 2, 1, 3)
            v = (value @ v_w.T + v_b).reshape(B, S_k, H, d).transpose(0, 2, 1, 3)
            q = apply_rope(q) * d ** (-0.5)
            k = apply_rope(k)
            q_pos = jnp.arange(S_q)[:, None]
            offsets = jnp.arange(-W, 1)[None, :]
            idx = q_pos + offsets
            local_mask = (idx < 0) | (idx >= S_k)
            gidx = jnp.clip(idx, 0, S_k - 1)
            k_win = k[:, :, gidx, :]
            v_win = v[:, :, gidx, :]
            scores = jnp.einsum('bhqd,bhqwd->bhqw', q, k_win)
            mask = local_mask[None, None, :, :]
            scores = jnp.where(mask, -jnp.inf, scores)
            m = jnp.max(scores, axis=-1, keepdims=True)
            m = jnp.where(jnp.isfinite(m), m, 0.0)
            e = jnp.exp(scores - m)
            denom = jnp.sum(e, axis=-1, keepdims=True)
            probs = jnp.where(denom > 0, e / jnp.where(denom > 0, denom, 1.0), 0.0)
            ctx = jnp.einsum('bhqw,bhqwd->bhqd', probs, v_win)
            ctx = ctx.transpose(0, 2, 1, 3).reshape(B, S_q, D)
            return ctx @ o_w.T + o_b
        key = jax.random.key(seed)
        ks = jax.random.split(key, 12)
        B, S, D = (1, 256, EMBED_DIM)
        scale = 1.0 / np.sqrt(D)
        inp = {'query': jax.random.normal(ks[0], (B, S, D), jnp.float32), 'key': jax.random.normal(ks[1], (B, S, D), jnp.float32), 'value': jax.random.normal(ks[2], (B, S, D), jnp.float32), 'q_w': jax.random.normal(ks[3], (D, D), jnp.float32) * scale, 'q_b': jax.random.normal(ks[4], (D,), jnp.float32) * 0.01, 'k_w': jax.random.normal(ks[5], (D, D), jnp.float32) * scale, 'k_b': jax.random.normal(ks[6], (D,), jnp.float32) * 0.01, 'v_w': jax.random.normal(ks[7], (D, D), jnp.float32) * scale, 'v_b': jax.random.normal(ks[8], (D,), jnp.float32) * 0.01, 'o_w': jax.random.normal(ks[9], (D, D), jnp.float32) * scale, 'o_b': jax.random.normal(ks[10], (D,), jnp.float32) * 0.01}
        return inp
    _L0_xattn_all = _L0_xattn_setup()
    _L0_xattn_in = {k: v for k, v in _L0_xattn_all.items() if k in ('q_w', 'q_b', 'k_w', 'k_b', 'v_w', 'v_b', 'o_w', 'o_b')}
    del _L0_xattn_all

    def _L0_ffn_setup():
        import jax, jax.numpy as jnp
        import numpy as np
        B, S, D = (1, 256, 128)
        E, K, F = (8, 2, 176)
        NS = 2
        SCALE = 2.5

        def _swiglu_mlp(x, wg, wu, wd):
            return jax.nn.silu(x @ wg) * (x @ wu) @ wd
        key = jax.random.key(seed)
        ks = jax.random.split(key, 8)
        s = 0.02
        return {'hidden_states': jax.random.normal(ks[0], (B, S, D), jnp.float32), 'gate_w': jax.random.normal(ks[1], (E, D), jnp.float32) * s, 'w_gate': jax.random.normal(ks[2], (E, D, F), jnp.float32) * s, 'w_up': jax.random.normal(ks[3], (E, D, F), jnp.float32) * s, 'w_down': jax.random.normal(ks[4], (E, F, D), jnp.float32) * s, 'sw_gate': jax.random.normal(ks[5], (D, F * NS), jnp.float32) * s, 'sw_up': jax.random.normal(ks[6], (D, F * NS), jnp.float32) * s, 'sw_down': jax.random.normal(ks[7], (F * NS, D), jnp.float32) * s}
    _L0_ffn_all = _L0_ffn_setup()
    _L0_ffn_in = {k: v for k, v in _L0_ffn_all.items() if k in ('gate_w', 'w_gate', 'w_up', 'w_down', 'sw_gate', 'sw_up', 'sw_down')}
    del _L0_ffn_all
    return {'x': x, 'ctx_1024': ctx_1024, 'L0_xattn_q_w': _L0_xattn_in['q_w'], 'L0_xattn_q_b': _L0_xattn_in['q_b'], 'L0_xattn_k_w': _L0_xattn_in['k_w'], 'L0_xattn_k_b': _L0_xattn_in['k_b'], 'L0_xattn_v_w': _L0_xattn_in['v_w'], 'L0_xattn_v_b': _L0_xattn_in['v_b'], 'L0_xattn_o_w': _L0_xattn_in['o_w'], 'L0_xattn_o_b': _L0_xattn_in['o_b'], 'L0_ffn_gate_w': _L0_ffn_in['gate_w'], 'L0_ffn_w_gate': _L0_ffn_in['w_gate'], 'L0_ffn_w_up': _L0_ffn_in['w_up'], 'L0_ffn_w_down': _L0_ffn_in['w_down'], 'L0_ffn_sw_gate': _L0_ffn_in['sw_gate'], 'L0_ffn_sw_up': _L0_ffn_in['sw_up'], 'L0_ffn_sw_down': _L0_ffn_in['sw_down']}

def reference(x, ctx_1024, L0_xattn_q_w, L0_xattn_q_b, L0_xattn_k_w, L0_xattn_k_b, L0_xattn_v_w, L0_xattn_v_b, L0_xattn_o_w, L0_xattn_o_b, L0_ffn_gate_w, L0_ffn_w_gate, L0_ffn_w_up, L0_ffn_w_down, L0_ffn_sw_gate, L0_ffn_sw_up, L0_ffn_sw_down):
    import jax
    import jax.numpy as jnp

    def _L0_xattn_ref(query, key, value, q_w, q_b, k_w, k_b, v_w, v_b, o_w, o_b):
        import jax, jax.numpy as jnp
        import numpy as np
        EMBED_DIM = 128
        NUM_HEADS = 16
        HEAD_DIM = EMBED_DIM // NUM_HEADS
        WINDOW = 64

        def apply_rope(x):
            B, H, S, d = x.shape
            half = d // 2
            pos = jnp.arange(S, dtype=x.dtype)
            freqs = 1.0 / 10000.0 ** (jnp.arange(half, dtype=x.dtype) / half)
            ang = pos[:, None] * freqs[None, :]
            cos, sin = (jnp.cos(ang), jnp.sin(ang))
            x1, x2 = (x[..., :half], x[..., half:])
            return jnp.concatenate([x1 * cos - x2 * sin, x1 * sin + x2 * cos], axis=-1)

        def _forward(query, key, value, q_w, q_b, k_w, k_b, v_w, v_b, o_w, o_b):
            B, S_q, D = query.shape
            S_k = key.shape[1]
            H, d, W = (NUM_HEADS, HEAD_DIM, WINDOW)
            q = (query @ q_w.T + q_b).reshape(B, S_q, H, d).transpose(0, 2, 1, 3)
            k = (key @ k_w.T + k_b).reshape(B, S_k, H, d).transpose(0, 2, 1, 3)
            v = (value @ v_w.T + v_b).reshape(B, S_k, H, d).transpose(0, 2, 1, 3)
            q = apply_rope(q) * d ** (-0.5)
            k = apply_rope(k)
            q_pos = jnp.arange(S_q)[:, None]
            offsets = jnp.arange(-W, 1)[None, :]
            idx = q_pos + offsets
            local_mask = (idx < 0) | (idx >= S_k)
            gidx = jnp.clip(idx, 0, S_k - 1)
            k_win = k[:, :, gidx, :]
            v_win = v[:, :, gidx, :]
            scores = jnp.einsum('bhqd,bhqwd->bhqw', q, k_win)
            mask = local_mask[None, None, :, :]
            scores = jnp.where(mask, -jnp.inf, scores)
            m = jnp.max(scores, axis=-1, keepdims=True)
            m = jnp.where(jnp.isfinite(m), m, 0.0)
            e = jnp.exp(scores - m)
            denom = jnp.sum(e, axis=-1, keepdims=True)
            probs = jnp.where(denom > 0, e / jnp.where(denom > 0, denom, 1.0), 0.0)
            ctx = jnp.einsum('bhqw,bhqwd->bhqd', probs, v_win)
            ctx = ctx.transpose(0, 2, 1, 3).reshape(B, S_q, D)
            return ctx @ o_w.T + o_b
        return _forward(query, key, value, q_w, q_b, k_w, k_b, v_w, v_b, o_w, o_b)

    def _L0_ffn_ref(hidden_states, gate_w, w_gate, w_up, w_down, sw_gate, sw_up, sw_down):
        import jax, jax.numpy as jnp
        import numpy as np
        B, S, D = (1, 256, 128)
        E, K, F = (8, 2, 176)
        NS = 2
        SCALE = 2.5

        def _swiglu_mlp(x, wg, wu, wd):
            return jax.nn.silu(x @ wg) * (x @ wu) @ wd
        identity = hidden_states
        x = hidden_states.reshape(-1, hidden_states.shape[-1])
        T = x.shape[0]
        logits = x.astype(jnp.float32) @ gate_w.astype(jnp.float32).T
        scores = jax.nn.softmax(logits, axis=-1)
        topk_w, topk_i = jax.lax.top_k(scores, K)
        topk_w = topk_w / (topk_w.sum(-1, keepdims=True) + 1e-20) * SCALE
        combine = jnp.zeros((T, E), jnp.float32).at[jnp.arange(T)[:, None], topk_i].set(topk_w)
        g = jax.nn.silu(jnp.einsum('td,edf->etf', x, w_gate)) * jnp.einsum('td,edf->etf', x, w_up)
        expert_out = jnp.einsum('etf,efd->etd', g, w_down)
        y = jnp.einsum('te,etd->td', combine, expert_out).astype(x.dtype)
        y = y.reshape(identity.shape)
        return y + _swiglu_mlp(identity, sw_gate, sw_up, sw_down)
    x = x + _L0_xattn_ref(_layernorm(x, axis=-1), ctx_1024, ctx_1024, L0_xattn_q_w, L0_xattn_q_b, L0_xattn_k_w, L0_xattn_k_b, L0_xattn_v_w, L0_xattn_v_b, L0_xattn_o_w, L0_xattn_o_b)
    x = x + _L0_ffn_ref(_layernorm(x, axis=-1), L0_ffn_gate_w, L0_ffn_w_gate, L0_ffn_w_up, L0_ffn_w_down, L0_ffn_sw_gate, L0_ffn_sw_up, L0_ffn_sw_down)
    return x

_drawn_inputs = setup_inputs


def setup_inputs(seed=0):
    import zlib

    import numpy as np

    out = dict(_drawn_inputs(seed))
    spreads = {}
    factors = {'L0_xattn_q_b': 8.0,
     'L0_xattn_k_b': 28.362,
     'L0_xattn_v_b': 8.0,
     'L0_xattn_o_b': 5.165,
     'L0_ffn_gate_w': 5.558,
     'L0_ffn_w_gate': 4.865,
     'L0_ffn_w_up': 4.818,
     'L0_ffn_w_down': 4.828,
     'L0_ffn_sw_gate': 6.106,
     'L0_ffn_sw_up': 6.088,
     'L0_ffn_sw_down': 6.086}
    for name, (base, spread) in spreads.items():
        noise = np.random.default_rng([zlib.crc32(name.encode()), seed]).standard_normal(out[name].shape)
        drawn = base * np.exp(spread * noise) if base else spread * noise
        out[name] = jnp.asarray(drawn.astype(out[name].dtype))
    for name, factor in factors.items():
        out[name] = (out[name] * factor).astype(out[name].dtype)
    return out
```

```python
from contextlib import ExitStack

import numpy as np

import concourse.bass as bass
from concourse import mybir

F32 = mybir.dt.float32
F32R = mybir.dt.float32r
BF16 = mybir.dt.bfloat16
ALU = mybir.AluOpType
ACT = mybir.ActivationFunctionType
AX = mybir.AxisListType

P = 128
D = 128
NB = 2
S = 512
S_CTX = 77
WINDOW = 64
H = 16
DH = D // H
E = 8
F = 176
FS = 2 * F
NSEG = (E * F + FS) // FS
HID = NSEG * FS
NCH = -(-HID // P)
LASTC = HID - (NCH - 1) * P
LN_EPS = 1e-5
TOP_SCALE = 2.5
TOP_EPS = 1e-20
MASKED = -1e30

TILES = [
    [(0, 0, 128)],
    [(1, 0, 128)],
    [(0, 128, 32), (1, 128, 32), (0, 160, 64)],
    [(0, 224, 128)],
    [(0, 352, 128)],
    [(0, 480, 32), (1, 160, 96)],
    [(1, 256, 128)],
    [(1, 384, 128)],
]
NT = len(TILES)
GROUPS = [[3, 4, 5, 6], [7, 0, 1, 2]]
ATT_ROWS = [128, 128, 64]
NQ = sum(ATT_ROWS)
QCOL = [0, 128, 256]

AW = {}
_at = 0
for _n, _w in (("ctxT", NB * S_CTX), ("kw", D), ("kws", D), ("vw", D), ("qw", D), ("qws", D),
               ("bias", 4), ("ow", D), ("gw", E)):
    AW[_n] = (_at, _at + _w)
    _at += _w
AW_W = _at
CT = {}
_at = 0
for _n, _w in (("ident", P), ("cosk", NB * S_CTX), ("sink", NB * S_CTX), ("m4", 4), ("valid", 1),
               ("half", 8), ("cosq", NQ), ("sinq", NQ), ("thr", E * E)):
    CT[_n] = (_at, _at + _w)
    _at += _w
CT_W = _at
CB_W = P + 2 * S_CTX


def build(nc, x, attw, consts, cbf, rows, wgu, wdn, out):
    with ExitStack() as ctx:
        def sb(name, shape, dt=F32):
            return ctx.enter_context(nc.sbuf_tensor(name, shape, dt))

        def sem(name):
            return ctx.enter_context(nc.semaphore(name))

        xr = sb("xr", [P, NT, D])
        attw_sb = sb("attw_sb", [P, AW_W])
        ct = sb("ct", [P, CT_W])
        cb = sb("cb", [P, CB_W], BF16)
        ob = sb("ob", [P, D])
        vb = sb("vb", [P, D])
        w = sb("w", [P, NSEG, 2 * FS])
        w_hi = sb("w_hi", [P, NSEG, 2 * FS], F32R)
        w_lo = sb("w_lo", [P, NSEG, 2 * FS], F32R)
        wd = sb("wd", [P, NCH, D])
        wd_hi = sb("wd_hi", [P, NCH, D], F32R)
        wd_lo = sb("wd_lo", [P, NCH, D], F32R)
        gw_hi = sb("gw_hi", [P, E], F32R)
        gw_lo = sb("gw_lo", [P, E], F32R)

        stats = sb("stats", [P, NT + 3, 6])
        mv = sb("mv", [P, NT + 3, 2])
        rstd = sb("rstd", [P, NT + 3])
        xn = sb("xn", [P, NT + 3, D])
        xn1T = sb("xn1T", [P, NQ])
        q1 = sb("q1", [P, NQ])
        q2 = sb("q2", [P, NQ])
        qT = sb("qT", [P, NQ])
        k1 = sb("k1", [P, NB * S_CTX])
        k2 = sb("k2", [P, NB * S_CTX])
        kT = sb("kT", [P, NB * S_CTX])
        kbd = sb("kbd", [P, NB, 4, S_CTX])
        vaug = sb("vaug", [S_CTX, NB, H, DH + 1])
        smax = sb("smax", [P, 6, 8])
        prob = sb("prob", [P, 6, 8, S_CTX])
        probT = sb("probT", [S_CTX, 2, 4, P])
        rden = sb("rden", [P, 3, H])
        cn = sb("cn", [P, 3, D])
        cT = sb("cT", [P, 3, P])

        lmax = sb("lmax", [P, 2, 4])
        lexp = sb("lexp", [P, 2, 4, E])
        lsum = sb("lsum", [P, 2, 4])
        lrec = sb("lrec", [P, 2, 4])
        lp = sb("lp", [P, 2, 4, E])
        ldif = sb("ldif", [P, 2, 4, E, E])
        lrank = sb("lrank", [P, 2, 4, E])
        lsel = sb("lsel", [P, 2, 4, E])
        tsum = sb("tsum", [P, 2, 4])
        trec = sb("trec", [P, 2, 4])
        comb = sb("comb", [P, 2, 4, E])

        xT_hi = sb("xT_hi", [P, 2, 4 * P], F32R)
        xT_lo = sb("xT_lo", [P, 2, 4 * P], F32R)
        xrT = sb("xrT", [P, 2, 4 * P])
        sg = sb("sg", [P, 3, FS])
        hid = sb("hid", [P, 2, 4, HID])
        hT_hi = sb("hT_hi", [P, 3, 4 * P], F32R)
        hT_lo = sb("hT_lo", [P, 3, 4 * P], F32R)
        y = sb("y", [P, 2, 4 * P])

        bank = [ctx.enter_context(nc.psum_tensor(f"bank{i}", [P, 512], F32)) for i in range(8)]
        gate_ps, up_ps, turn_ps, down_ps = bank[0:2], bank[2:4], bank[4:6], bank[6]
        scores_ps = [bank[4:6], bank[6:8]]
        ctx_ps = [bank[7], bank[5]]
        pT_ps, ctxT_ps = bank[6], bank[4]

        ld_xa, ld_xb = sem("ld_xa"), sem("ld_xb")
        ld_attw, ld_const, ld_cb, ld_ob, ld_vb = (sem(n) for n in ("ld_attw", "ld_const", "ld_cb", "ld_ob", "ld_vb"))
        ld_w = [sem(f"ld_w{s}") for s in range(NSEG)]
        ld_wd = sem("ld_wd")
        stored = sem("stored")
        dve_raw, pool_raw, act_raw = sem("dve_raw"), sem("pool_raw"), sem("act_raw")
        var_ready, rstd_ready = sem("var_ready"), sem("rstd_ready")
        pool_xr = sem("pool_xr")
        pool_w, pool_wd, pool_gw, pool_kbd = sem("pool_w"), sem("pool_wd"), sem("pool_gw"), sem("pool_kbd")
        w0_hi, w0_lo = sem("w0_hi"), sem("w0_lo")
        xn1_ready, xn1T_ps, xn1T_ready = sem("xn1_ready"), sem("xn1T_ps"), sem("xn1T_ready")
        k_ps, v_ps, q_ps = sem("k_ps"), sem("v_ps"), sem("q_ps")
        kT_ready, v_ready, q_ready = sem("kT_ready"), sem("v_ready"), sem("q_ready")
        scores_done, scores_read, prob_ready = sem("scores_done"), sem("scores_read"), sem("prob_ready")
        pT_done, pT_read, ctx_done = sem("pT_done"), sem("pT_read"), sem("ctx_done")
        cn_ready, cT_ps, cT_ready, o_ps, x1_ready = (sem(n) for n in ("cn_ready", "cT_ps", "cT_ready", "o_ps", "x1_ready"))
        xn_ready = sem("xn_ready")
        xT_ps, xThi_ready, xTlo_ready = sem("xT_ps"), sem("xThi_ready"), sem("xTlo_ready")
        xrT_ps, xrT_ready = sem("xrT_ps"), sem("xrT_ready")
        logit_ps, lsub_ready, lexp_ready, comb_ready = sem("logit_ps"), sem("lsub_ready"), sem("lexp_ready"), sem("comb_ready")
        gate_done, up_done, silu_done, hid_done = sem("gate_done"), sem("up_done"), sem("silu_done"), sem("hid_done")
        turned, hi_done, lo_done, down_done, y_ready = (sem(n) for n in ("turned", "hi_done", "lo_done", "down_done", "y_ready"))

        aw = {n: attw_sb[:, a:b] for n, (a, b) in AW.items()}
        cc = {n: ct[:, a:b] for n, (a, b) in CT.items()}
        ident = cc["ident"]
        identb = cb[:, 0:P]
        maskb = [cb[:, P:P + S_CTX], cb[:, P:P + S_CTX], cb[:, P + S_CTX:P + 2 * S_CTX]]

        def width(c):
            return LASTC if c == NCH - 1 else P

        def seg_of_chunk(c):
            return (c * P + width(c) - 1) // FS

        block = ctx.enter_context(nc.Block())

        @block.sync
        def _(sp):
            sp.dma_start(xr[:, 0:3, :], x[:, 0:3, :]).then_inc(ld_xa, 16)
            sp.dma_start(ct[:], consts).then_inc(ld_const, 16)
            sp.dma_start(xr[:, 3:8, :], x[:, 3:8, :]).then_inc(ld_xb, 16)
            for s in range(NSEG):
                sp.dma_start(w[:, s, :], wgu[:, s, :]).then_inc(ld_w[s], 16)
            sp.dma_start(wd[:], wdn).then_inc(ld_wd, 16)
            for g in range(2):
                for half in range(2):
                    sp.wait_ge(y_ready, 2 * g + half + 1)
                    cols = slice(256 * half, 256 * half + 256)
                    sp.dma_start(out[:, g, cols], y[:, g, cols]).then_inc(stored, 16)
            sp.wait_ge(stored, 16 * 4)

        @block.gpsimd
        def _(pool):
            n_raw = [0]

            def then(ins):
                n_raw[0] += 1
                ins.then_inc(pool_raw, 1)
                pool.wait_ge(pool_raw, n_raw[0])

            n_var = [0]

            def make_rstd(a, b):
                n_var[0] += 1
                pool.wait_ge(var_ready, n_var[0])
                then(nc.gpsimd.tensor_scalar(rstd[:, a:b], mv[:, a:b, 1], LN_EPS, None, ALU.add))
                nc.gpsimd.tensor_tensor(rstd[:, a:b], rstd[:, a:b], cc["half"][:, 0:b - a], ALU.pow).then_inc(rstd_ready, 1)

            def split(dst_hi, dst_lo, src, done):
                then(nc.gpsimd.tensor_copy(dst_hi, src))
                nc.gpsimd.tensor_tensor(dst_lo, src, dst_hi.bitcast(F32), ALU.subtract).then_inc(done, 1)

            def add_ob(a, b):
                nc.gpsimd.tensor_tensor(xr[:, a:b, :], xr[:, a:b, :],
                                        ob[:, None, :].to_broadcast([P, b - a, D]), ALU.add).then_inc(pool_xr, 1)

            pool.wait_ge(ld_const, 16)
            make_rstd(NT, NT + 3)
            pool.wait_ge(ld_ob, 16)
            pool.wait_ge(ld_xb, 16)
            add_ob(3, 8)
            pool.wait_ge(xn1_ready, 1)
            add_ob(0, 3)
            make_rstd(3, 8)
            pool.wait_ge(ld_attw, 16)
            split(gw_hi[:], gw_lo[:], aw["gw"], pool_gw)
            for s in range(1, NSEG):
                pool.wait_ge(ld_w[s], 16)
                split(w_hi[:, s, :], w_lo[:, s, :], w[:, s, :], pool_w)
            pool.wait_ge(ld_wd, 16)
            make_rstd(0, 1)
            split(wd_hi[:, 0:7, :], wd_lo[:, 0:7, :], wd[:, 0:7, :], pool_wd)
            make_rstd(1, 2)
            split(wd_hi[:, 7:, :], wd_lo[:, 7:, :], wd[:, 7:, :], pool_wd)
            make_rstd(2, 3)

        @block.scalar
        def _(act):
            act.dma_start(attw_sb[:], attw).then_inc(ld_attw, 16)
            act.dma_start(cb[:], cbf).then_inc(ld_cb, 16)
            act.dma_start(ob[:], rows[0:1, :].partition_broadcast(P)).then_inc(ld_ob, 16)
            act.dma_start(vb[:], rows[1:2, :].partition_broadcast(P)).then_inc(ld_vb, 16)

            act.wait_ge(xn1T_ps, 1)
            nc.scalar.copy(xn1T[:], bank[0][:, 0:NQ]).then_inc(xn1T_ready, 1)
            act.wait_ge(ld_w[0], 16)
            nc.scalar.copy(w_hi[:, 0, :], w[:, 0, :]).then_inc(w0_hi, 1)

            def xT_high(g):
                act.wait_ge(xT_ps, g + 1)
                nc.scalar.copy(xT_hi[:, g, :], bank[0 if g == 0 else 4][:, 0:512]).then_inc(xThi_ready, 1)
                act.wait_ge(xrT_ps, g + 1)
                nc.scalar.copy(xrT[:, g, :], bank[2 if g == 0 else 5][:, 0:512]).then_inc(xrT_ready, 1)

            def route_exp(g):
                act.wait_ge(lsub_ready, g + 1)
                nc.scalar.activation(lexp[:, g], lexp[:, g], ACT.Exp).then_inc(lexp_ready, 1)

            def attend_exp(a):
                r = ATT_ROWS[a // 2]
                act.wait_ge(scores_read, a + 1)
                nc.scalar.activation(prob[0:r, a], prob[0:r, a], ACT.Exp).then_inc(prob_ready, 1)

            for a in range(3):
                attend_exp(a)
            xT_high(0)
            attend_exp(3)
            route_exp(0)
            for a in range(4, 6):
                attend_exp(a)

            def silu(n):
                act.wait_ge(gate_done, n + 1)
                if n >= 3:
                    act.wait_ge(hid_done, n - 2)
                nc.scalar.activation(sg[:, n % 3, :], gate_ps[n % 2][:, 0:FS], ACT.Silu).then_inc(silu_done, 1)

            def probT_copy(b):
                r = ATT_ROWS[b // 4]
                act.wait_ge(pT_done, b + 1)
                if b >= 2:
                    act.wait_ge(ctx_done, b - 1)
                nc.scalar.copy(probT[:, b % 2, :, 0:r],
                               pT_ps[0:S_CTX, :].rearrange("k (h q) -> k h q", h=4)[:, :, 0:r]).then_inc(pT_read, 1)

            def ctxT_copy(t):
                act.wait_ge(cT_ps, t + 1)
                nc.scalar.copy(cT[:, t, 0:ATT_ROWS[t]], ctxT_ps[:, 0:ATT_ROWS[t]]).then_inc(cT_ready, 1)

            def hidT_high(m):
                wc = width(m % NCH)
                act.wait_ge(turned, m + 1)
                if m >= 3:
                    act.wait_ge(down_done, m - 2)
                nc.scalar.copy(hT_hi[0:wc, m % 3, :], turn_ps[m % 2][0:wc, :]).then_inc(hi_done, 1)

            for n in range(20):
                if n < 12:
                    probT_copy(n)
                silu(n)
                if n in (6, 10, 14):
                    ctxT_copy((n - 6) // 4)
            xT_high(1)
            route_exp(1)
            for step in SECOND:
                if step[0] == "unit":
                    silu(step[1])
                else:
                    hidT_high(step[1])

        @block.vector
        def _(dve):
            n_raw = [0]

            def then(ins):
                n_raw[0] += 1
                ins.then_inc(dve_raw, 1)
                dve.wait_ge(dve_raw, n_raw[0])

            n_rstd = [0]

            def norm_stats(tiles, at):
                for i, t in enumerate(tiles):
                    last = nc.vector.bn_stats(stats[:, at + i, :], xr[:, t, :])
                then(last)
                for i in range(len(tiles)):
                    last = nc.vector.bn_aggr(mv[:, at + i, :], stats[:, at + i, :])
                last.then_inc(var_ready, 1)

            def normalise(tiles, at):
                n_rstd[0] += 1
                dve.wait_ge(rstd_ready, n_rstd[0])
                for i, t in enumerate(tiles):
                    last = nc.vector.tensor_scalar(xn[:, at + i, :], xr[:, t, :], mv[:, at + i, 0:1],
                                                   rstd[:, at + i:at + i + 1], ALU.subtract, ALU.mult)
                return last

            nc.vector.memset(vaug[:], 1.0)
            dve.wait_ge(ld_xa, 16)
            norm_stats([0, 1, 2], NT)
            normalise([0, 1, 2], NT).then_inc(xn1_ready, 1)

            def rope(dst, a, b, in1, in2, bias1, bias2, cos, sin):
                nc.vector.scalar_tensor_tensor(out=a, in0=in1, scalar=bias1, in1=cos, op0=ALU.add, op1=ALU.mult)
                then(nc.vector.scalar_tensor_tensor(out=b, in0=in2, scalar=bias2, in1=sin, op0=ALU.add, op1=ALU.mult))
                return nc.vector.tensor_tensor(dst, a, b, ALU.add)

            dve.wait_ge(ld_attw, 16)
            dve.wait_ge(ld_const, 16)
            dve.wait_ge(k_ps, 1)
            nk = NB * S_CTX
            then(rope(kT[:], k1[:], k2[:], bank[1][:, 0:nk], bank[1][:, nk:2 * nk],
                      aw["bias"][:, 2:3], aw["bias"][:, 3:4], cc["cosk"], cc["sink"]))
            for b in range(NB):
                last = nc.vector.tensor_tensor(kbd[:, b], kT[:, None, b * S_CTX:(b + 1) * S_CTX].to_broadcast([P, 4, S_CTX]),
                                               cc["m4"][:, :, None].to_broadcast([P, 4, S_CTX]), ALU.mult)
            last.then_inc(kT_ready, 1)
            dve.wait_ge(q_ps, 1)
            rope(qT[:], q1[:], q2[:], bank[2][:, 0:NQ], bank[3][:, 0:NQ],
                 aw["bias"][:, 0:1], aw["bias"][:, 1:2], cc["cosq"], cc["sinq"]).then_inc(q_ready, 1)
            dve.wait_ge(v_ps, 1)
            dve.wait_ge(ld_vb, 16)
            for b in range(NB):
                last = nc.vector.tensor_tensor(
                    vaug[:, b, :, 0:DH], bank[7][0:S_CTX, b * D:(b + 1) * D].rearrange("k (h d) -> k h d", h=H),
                    vb[0:S_CTX, :].rearrange("k (h d) -> k h d", h=H), ALU.add)
            last.then_inc(v_ready, 1)

            dve.wait_ge(pool_xr, 1)
            norm_stats([3, 4, 5, 6, 7], 3)

            def softmax_max(a):
                t, r = a // 2, ATT_ROWS[a // 2]
                dve.wait_ge(scores_done, a + 1)
                for j in range(2):
                    sc = scores_ps[a % 2][j][0:r, 0:4 * S_CTX].rearrange("q (h k) -> q h k", h=4)
                    last = nc.vector.tensor_reduce(smax[0:r, a, 4 * j:4 * j + 4], sc, AX.X, ALU.max)
                then(last)
                for j in range(2):
                    sc = scores_ps[a % 2][j][0:r, 0:4 * S_CTX].rearrange("q (h k) -> q h k", h=4)
                    last = nc.vector.tensor_tensor(
                        prob[0:r, a, 4 * j:4 * j + 4, :], sc,
                        smax[0:r, a, 4 * j:4 * j + 4, None].to_broadcast([r, 4, S_CTX]), ALU.subtract)
                last.then_inc(scores_read, 1)

            def xT_low(g):
                dve.wait_ge(xThi_ready, g + 1)
                nc.vector.tensor_tensor(xT_lo[:, g, :], bank[0 if g == 0 else 4][:, 0:512],
                                        xT_hi[:, g, :].bitcast(F32), ALU.subtract).then_inc(xTlo_ready, 1)

            def route_sub(g):
                dve.wait_ge(logit_ps, g + 1)
                lg = bank[1 if g == 0 else 7][:, 0:4 * E].rearrange("p (t e) -> p t e", t=4)
                then(nc.vector.tensor_reduce(lmax[:, g, :], lg, AX.X, ALU.max))
                nc.vector.tensor_tensor(lexp[:, g], lg, lmax[:, g, :, None].to_broadcast([P, 4, E]),
                                        ALU.subtract).then_inc(lsub_ready, 1)

            def route(g):
                dve.wait_ge(lexp_ready, g + 1)
                then(nc.vector.tensor_reduce(lsum[:, g, :], lexp[:, g], AX.X, ALU.add))
                then(nc.vector.reciprocal(lrec[:, g, :], lsum[:, g, :]))
                then(nc.vector.tensor_tensor(lp[:, g], lexp[:, g], lrec[:, g, :, None].to_broadcast([P, 4, E]), ALU.mult))
                then(nc.vector.tensor_tensor(ldif[:, g], lp[:, g, :, None, :].to_broadcast([P, 4, E, E]),
                                             lp[:, g, :, :, None].to_broadcast([P, 4, E, E]), ALU.subtract))
                then(nc.vector.tensor_tensor(ldif[:, g].rearrange("p t e j -> p t (e j)"),
                                             ldif[:, g].rearrange("p t e j -> p t (e j)"),
                                             cc["thr"][:, None, :].to_broadcast([P, 4, E * E]), ALU.is_ge))
                then(nc.vector.tensor_reduce(lrank[:, g], ldif[:, g], AX.X, ALU.add))
                then(nc.vector.scalar_tensor_tensor(out=lsel[:, g], in0=lrank[:, g], scalar=1.5, in1=lp[:, g],
                                                    op0=ALU.is_lt, op1=ALU.mult))
                then(nc.vector.tensor_reduce(tsum[:, g, :], lsel[:, g], AX.X, ALU.add))
                then(nc.vector.tensor_scalar(tsum[:, g, :], tsum[:, g, :], TOP_EPS, None, ALU.add))
                then(nc.vector.reciprocal(trec[:, g, :], tsum[:, g, :]))
                nc.vector.scalar_tensor_tensor(out=comb[:, g], in0=lsel[:, g], scalar=TOP_SCALE,
                                               in1=trec[:, g, :, None].to_broadcast([P, 4, E]),
                                               op0=ALU.mult, op1=ALU.mult).then_inc(comb_ready, 1)

            softmax_max(0)
            normalise([3, 4, 5, 6, 7], 3).then_inc(xn_ready, 1)
            softmax_max(1)
            dve.wait_ge(w0_hi, 1)
            nc.vector.tensor_tensor(w_lo[:, 0, :], w[:, 0, :], w_hi[:, 0, :].bitcast(F32), ALU.subtract).then_inc(w0_lo, 1)
            softmax_max(2)
            xT_low(0)
            softmax_max(3)
            route_sub(0)
            softmax_max(4)
            route(0)
            softmax_max(5)

            def hidden(n):
                g, s, i = n // 20, n % 20 // 4, n % 4
                dve.wait_ge(silu_done, n + 1)
                dve.wait_ge(up_done, n + 1)
                if s == 0 and i == 0:
                    dve.wait_ge(comb_ready, g + 1)
                h = hid[:, g, i, s * FS:(s + 1) * FS]
                if s == NSEG - 1:
                    nc.vector.tensor_tensor(h, sg[:, n % 3, :], up_ps[n % 2][:, 0:FS], ALU.mult).then_inc(hid_done, 1)
                    return
                for j in range(2):
                    cols = slice(j * F, (j + 1) * F)
                    last = nc.vector.scalar_tensor_tensor(
                        out=h[:, cols], in0=sg[:, n % 3, cols], scalar=comb[:, g, i, 2 * s + j:2 * s + j + 1],
                        in1=up_ps[n % 2][:, cols], op0=ALU.mult, op1=ALU.mult)
                last.then_inc(hid_done, 1)

            def ctx_norm(t):
                r = ATT_ROWS[t]
                dve.wait_ge(ctx_done, 4 * t + 4)
                cv = ctx_ps[t % 2][0:r, 0:H * (DH + 1)].rearrange("q (h d) -> q h d", h=H)
                then(nc.vector.reciprocal(rden[0:r, t, :], cv[:, :, DH]))
                nc.vector.tensor_tensor(cn[0:r, t, :].rearrange("q (h d) -> q h d", h=H), cv[:, :, 0:DH],
                                        rden[0:r, t, :, None].to_broadcast([r, H, DH]), ALU.mult).then_inc(cn_ready, 1)

            def add_attention(t):
                r = ATT_ROWS[t]
                dve.wait_ge(o_ps, t + 1)
                dve.wait_ge(pool_xr, 2)
                scalar = 1.0 if t < 2 else cc["valid"][0:r, :]
                then(nc.vector.scalar_tensor_tensor(out=xr[0:r, t, :], in0=ctxT_ps[0:r, P:P + D], scalar=scalar,
                                                    in1=xr[0:r, t, :], op0=ALU.mult, op1=ALU.add))
                norm_stats([t], t)

            for n in range(20):
                hidden(n)
                if n in (4, 8, 12):
                    ctx_norm((n - 4) // 4)
                if n in (7, 11, 15):
                    add_attention((n - 7) // 4)
                if n in (8, 12, 16):
                    last = normalise([(n - 8) // 4], (n - 8) // 4)
            last.then_inc(xn_ready, 1)
            xT_low(1)
            route_sub(1)
            route(1)

            def hidT_low(m):
                wc = width(m % NCH)
                dve.wait_ge(hi_done, m + 1)
                if m >= 3:
                    dve.wait_ge(down_done, m - 2)
                nc.vector.tensor_tensor(hT_lo[0:wc, m % 3, :], turn_ps[m % 2][0:wc, :],
                                        hT_hi[0:wc, m % 3, :].bitcast(F32), ALU.subtract).then_inc(lo_done, 1)

            def finish(g):
                dve.wait_ge(down_done, NCH * (g + 1))
                dve.wait_ge(xrT_ready, g + 1)
                for half in range(2):
                    cols = slice(256 * half, 256 * half + 256)
                    nc.vector.tensor_tensor(y[:, g, cols], down_ps[:, cols], xrT[:, g, cols], ALU.add).then_inc(y_ready, 1)

            for kind, n in SECOND:
                if kind == "unit":
                    hidden(n)
                else:
                    hidT_low(n)
                    if n % NCH == NCH - 1:
                        finish(n // NCH)

        @block.tensor
        def _(pe):
            pe.wait_ge(ld_const, 16)
            pe.wait_ge(ld_attw, 16)
            nk = NB * S_CTX
            nc.tensor.matmul(bank[1][:, 0:nk], aw["kw"], aw["ctxT"], start=True, stop=True)
            nc.tensor.matmul(bank[1][:, nk:2 * nk], aw["kws"], aw["ctxT"], start=True, stop=True).then_inc(k_ps, 1)
            for b in range(NB):
                last = nc.tensor.matmul(bank[7][0:S_CTX, b * D:(b + 1) * D], aw["ctxT"][:, b * S_CTX:(b + 1) * S_CTX],
                                        aw["vw"], start=True, stop=True)
            last.then_inc(v_ps, 1)
            pe.wait_ge(xn1_ready, 1)
            for t in range(3):
                r = ATT_ROWS[t]
                last = nc.tensor.transpose(bank[0][:, QCOL[t]:QCOL[t] + r], xn[0:r, NT + t, :], ident[0:r, 0:r])
            last.then_inc(xn1T_ps, 1)
            pe.wait_ge(xn1T_ready, 1)
            nc.tensor.matmul(bank[2][:, 0:NQ], aw["qw"], xn1T[:], start=True, stop=True)
            nc.tensor.matmul(bank[3][:, 0:NQ], aw["qws"], xn1T[:], start=True, stop=True).then_inc(q_ps, 1)

            def scores(a):
                t, r = a // 2, ATT_ROWS[a // 2]
                if a == 1:
                    pe.wait_ge(v_ready, 1)
                if a >= 2:
                    pe.wait_ge(scores_read, a - 1)
                for j in range(2):
                    nc.tensor.matmul(scores_ps[a % 2][j][0:r, 0:4 * S_CTX], identb[0:r, 0:r],
                                     maskb[t][0:r, None, :].to_broadcast([r, 4, S_CTX]), start=True, stop=False,
                                     skip_group_check=True)
                for j in range(2):
                    g = 2 * (a % 2) + j
                    rows_ = slice(32 * g, 32 * g + 32)
                    for b, q0, q1_ in ([(t, 0, 128)] if t < 2 else [(0, 0, 32), (1, 32, 64)]):
                        last = nc.tensor.matmul(scores_ps[a % 2][j][q0:q1_, 0:4 * S_CTX],
                                                qT[rows_, QCOL[t] + q0:QCOL[t] + q1_],
                                                kbd[rows_, b].rearrange("p h k -> p (h k)"), start=False, stop=True,
                                                skip_group_check=True)
                last.then_inc(scores_done, 1)

            def turn_x(g):
                bx, br = (bank[0], bank[2]) if g == 0 else (bank[4], bank[5])
                for i, t in enumerate(GROUPS[g]):
                    last = nc.tensor.transpose(bx[:, i * P:(i + 1) * P], xn[:, t, :], ident)
                last.then_inc(xT_ps, 1)
                for i, t in enumerate(GROUPS[g]):
                    last = nc.tensor.transpose(br[:, i * P:(i + 1) * P], xr[:, t, :], ident)
                last.then_inc(xrT_ps, 1)

            def logits(g):
                bl = bank[1 if g == 0 else 7]
                pe.wait_ge(pool_gw, 1)
                pe.wait_ge(xThi_ready, g + 1)
                pe.wait_ge(xTlo_ready, g + 1)
                for i in range(4):
                    o, c = bl[:, i * E:(i + 1) * E], slice(i * P, (i + 1) * P)
                    nc.tensor.matmul(o, xT_hi[:, g, c], gw_hi[:], start=True, stop=False)
                    nc.tensor.matmul(o, xT_hi[:, g, c], gw_lo[:], start=False, stop=False)
                    last = nc.tensor.matmul(o, xT_lo[:, g, c], gw_hi[:], start=False, stop=True)
                last.then_inc(logit_ps, 1)

            pe.wait_ge(kT_ready, 1)
            pe.wait_ge(q_ready, 1)
            pe.wait_ge(ld_cb, 16)
            scores(0)
            scores(1)
            pe.wait_ge(xn_ready, 1)
            turn_x(0)
            scores(2)
            logits(0)
            scores(3)
            scores(4)
            scores(5)

            def stage_one(n):
                g, s, i = n // 20, n % 20 // 4, n % 4
                c = slice(i * P, (i + 1) * P)
                if s > 0 and i == 0:
                    pe.wait_ge(pool_w, s)
                if n == 0:
                    pe.wait_ge(w0_lo, 1)
                if n == 1:
                    pe.wait_ge(lsub_ready, 1)
                if n >= 2:
                    pe.wait_ge(silu_done, n - 1)
                for part in range(2):
                    ps = (gate_ps, up_ps)[part][n % 2][:, 0:FS]
                    cols = slice(part * FS, (part + 1) * FS)
                    if part and n == 0:
                        pe.wait_ge(xrT_ready, 1)
                    if part and n >= 2:
                        pe.wait_ge(hid_done, n - 1)
                    nc.tensor.matmul(ps, xT_hi[:, g, c], w_hi[:, s, cols], start=True, stop=False)
                    nc.tensor.matmul(ps, xT_hi[:, g, c], w_lo[:, s, cols], start=False, stop=False)
                    nc.tensor.matmul(ps, xT_lo[:, g, c], w_hi[:, s, cols], start=False,
                                     stop=True).then_inc((gate_done, up_done)[part], 1)

            def turn_probs(b):
                t, r = b // 4, ATT_ROWS[b // 4]
                a, j = b // 2, b % 2
                pe.wait_ge(prob_ready, a + 1)
                if b == 0:
                    pe.wait_ge(scores_read, 6)
                if b >= 1:
                    pe.wait_ge(pT_read, b)
                for hh in range(4):
                    last = nc.tensor.transpose(pT_ps[0:S_CTX, hh * P:hh * P + r],
                                               prob[0:r, a, 4 * j + hh, :], ident[0:r, 0:r])
                last.then_inc(pT_done, 1)

            def context(b):
                t = b // 4
                pe.wait_ge(pT_read, b + 1)
                if b % 4 == 0 and t == 2:
                    pe.wait_ge(cn_ready, 1)
                for hh in range(4):
                    h = 4 * (b % 4) + hh
                    for bb, q0, q1_ in ([(t, 0, 128)] if t < 2 else [(0, 0, 32), (1, 32, 64)]):
                        last = nc.tensor.matmul(ctx_ps[t % 2][q0:q1_, h * (DH + 1):(h + 1) * (DH + 1)],
                                                probT[:, b % 2, hh, q0:q1_], vaug[:, bb, h, :], start=True, stop=True)
                last.then_inc(ctx_done, 1)

            def turn_ctx(t):
                r = ATT_ROWS[t]
                pe.wait_ge(cn_ready, t + 1)
                if t >= 1:
                    pe.wait_ge(x1_done_of(t), x1_value(t))
                nc.tensor.transpose(ctxT_ps[:, 0:r], cn[0:r, t, :], ident[0:r, 0:r]).then_inc(cT_ps, 1)

            def project_out(t):
                r = ATT_ROWS[t]
                pe.wait_ge(cT_ready, t + 1)
                nc.tensor.matmul(ctxT_ps[0:r, P:P + D], cT[:, t, 0:r], aw["ow"], start=True, stop=True).then_inc(o_ps, 1)

            def x1_done_of(t):
                return var_ready

            def x1_value(t):
                return 2 + t

            for n in range(20):
                if n < 12:
                    turn_probs(n)
                stage_one(n)
                if 1 <= n < 13:
                    context(n - 1)
                if n in (5, 9, 13):
                    turn_ctx((n - 5) // 4)
                if n in (6, 10, 14):
                    project_out((n - 6) // 4)
                if n == 18:
                    pe.wait_ge(xn_ready, 2)
                    turn_x(1)
                if n == 19:
                    logits(1)

            def turn_hidden(m):
                g, c = divmod(m, NCH)
                wc = width(c)
                pe.wait_ge(hid_done, 20 * g + 4 * seg_of_chunk(c) + 4)
                if m < 2:
                    pe.wait_ge(xTlo_ready, 2)
                    pe.wait_ge(xrT_ready, 2)
                if m >= 2:
                    pe.wait_ge(lo_done, m - 1)
                for i in range(4):
                    last = nc.tensor.transpose(turn_ps[m % 2][0:wc, i * P:(i + 1) * P],
                                               hid[:, g, i, c * P:c * P + wc], ident)
                last.then_inc(turned, 1)

            def stage_two(m):
                g, c = divmod(m, NCH)
                wc = width(c)
                if c == 0 and g == 0:
                    pe.wait_ge(pool_wd, 1)
                if c == 7 and g == 0:
                    pe.wait_ge(pool_wd, 2)
                if c == 0 and g == 1:
                    pe.wait_ge(y_ready, 2)
                pe.wait_ge(hi_done, m + 1)
                s = m % 3
                nc.tensor.matmul(down_ps[:, :], wd_hi[0:wc, c, :], hT_hi[0:wc, s, :], start=(c == 0), stop=False)
                nc.tensor.matmul(down_ps[:, :], wd_lo[0:wc, c, :], hT_hi[0:wc, s, :], start=False, stop=False)
                pe.wait_ge(lo_done, m + 1)
                nc.tensor.matmul(down_ps[:, :], wd_hi[0:wc, c, :], hT_lo[0:wc, s, :], start=False,
                                 stop=(c == NCH - 1)).then_inc(down_done, 1)

            behind = None
            for kind, n in SECOND:
                if kind == "unit":
                    stage_one(n)
                else:
                    turn_hidden(n)
                if kind == "chunk" or kind == "unit":
                    if behind is not None and (kind == "chunk" or True):
                        stage_two(behind)
                        behind = None
                    if kind == "chunk":
                        behind = n
            stage_two(behind)


def second_half():
    steps, chunk = [], 0
    for n in range(20, 40):
        steps.append(("unit", n))
        done = (n - 20 + 1) // 4
        if chunk < NCH:
            steps.append(("chunk", chunk))
            chunk += 1
        elif ((chunk - NCH) * P + P - 1) // FS < (n - 20) // 4:
            steps.append(("chunk", chunk))
            chunk += 1
    steps += [("chunk", c) for c in range(chunk, 2 * NCH)]
    return steps


SECOND = second_half()


def positions(tile):
    return np.concatenate([np.arange(p, p + n) for _, p, n in TILES[tile]])


def rope_tables(pos, scale):
    half = DH // 2
    freqs = np.float32(1.0) / np.float32(10000.0) ** (np.arange(half, dtype=np.float32) / np.float32(half))
    ang = pos.astype(np.float32)[None, :] * freqs[:, None]
    cos, sin = np.cos(ang), np.sin(ang)
    cos = np.tile(np.concatenate([cos, cos]), (H, 1)) * scale
    sin = np.tile(np.concatenate([-sin, sin]), (H, 1)) * scale
    return cos.astype(np.float32), sin.astype(np.float32)


def constants():
    ct = np.zeros((P, CT_W), np.float32)

    def put(name, value):
        a, b = CT[name]
        ct[:, a:b] = value

    put("ident", np.eye(P))
    kpos = np.tile(np.arange(S_CTX), NB)
    cos, sin = rope_tables(kpos, 1.0)
    put("cosk", cos)
    put("sink", sin)
    qpos = np.concatenate([positions(t)[0:ATT_ROWS[t]] for t in range(3)])
    cos, sin = rope_tables(qpos, DH ** -0.5)
    put("cosq", cos)
    put("sinq", sin)
    rows = np.arange(P)
    put("m4", (rows % 32 // DH)[:, None] == np.arange(4)[None, :])
    valid = np.zeros(P)
    valid[0:64] = positions(2)[0:64] - WINDOW < S_CTX
    put("valid", valid[:, None])
    put("half", -0.5)
    e, j = np.meshgrid(np.arange(E), np.arange(E), indexing="ij")
    tiny = np.finfo(np.float32).tiny
    put("thr", np.where(j < e, 0.0, np.where(j > e, tiny, 2.0)).reshape(1, E * E))

    def mask(pos):
        k = np.arange(S_CTX)[None, :]
        return np.where((k <= pos[:, None]) & (k >= pos[:, None] - WINDOW), 0.0, MASKED)

    cbf = np.zeros((P, CB_W), np.float32)
    cbf[:, 0:P] = np.eye(P)
    cbf[:, P:P + S_CTX] = mask(positions(0))
    cbf[:, P + S_CTX:] = mask(positions(2))
    return ct, cbf


def kernel(**inputs):
    import ml_dtypes
    import concourse.bacc as bacc
    from concourse.bass_utils import run_bass_kernel_spmd

    a = {n: np.asarray(v) for n, v in inputs.items()}
    x = a["x"]
    xt = np.stack([np.concatenate([x[b, p:p + n] for b, p, n in runs]) for runs in TILES], axis=1)
    swap = np.arange(D).reshape(H, 2, DH // 2)[:, ::-1].reshape(D)
    att = {
        "ctxT": a["ctx_1024"].reshape(NB * S_CTX, D).T,
        "kw": a["L0_xattn_k_w"].T, "kws": a["L0_xattn_k_w"][swap].T, "vw": a["L0_xattn_v_w"].T,
        "qw": a["L0_xattn_q_w"].T, "qws": a["L0_xattn_q_w"][swap].T, "ow": a["L0_xattn_o_w"].T,
        "bias": np.stack([a["L0_xattn_q_b"], a["L0_xattn_q_b"][swap], a["L0_xattn_k_b"], a["L0_xattn_k_b"][swap]], axis=1),
        "gw": a["L0_ffn_gate_w"].T,
    }
    attw = np.concatenate([att[n] for n in AW], axis=1)

    def segments(experts, shared):
        e = experts.transpose(1, 0, 2).reshape(D, NSEG - 1, FS)
        return np.concatenate([e, shared[:, None, :]], axis=1)

    wgu = np.concatenate([segments(a["L0_ffn_w_gate"], a["L0_ffn_sw_gate"]),
                          segments(a["L0_ffn_w_up"], a["L0_ffn_sw_up"])], axis=2)
    down = np.concatenate([a["L0_ffn_w_down"].reshape(E * F, D), a["L0_ffn_sw_down"],
                           np.zeros((NCH * P - HID, D), np.float32)])
    wdn = down.reshape(NCH, P, D).transpose(1, 0, 2)
    rows = np.stack([a["L0_xattn_o_b"], a["L0_xattn_v_b"]])
    ct, cbf = constants()
    arrays = {"x_tiles": xt, "attw": attw, "consts": ct, "cbf": cbf.astype(ml_dtypes.bfloat16), "rows": rows,
              "wgu": wgu, "wdn": wdn}
    arrays = {n: np.ascontiguousarray(v) for n, v in arrays.items()}

    nc = bacc.Bacc("TRN2", target_bir_lowering=False, num_devices=1)
    args = [nc.dram_tensor(n, v.shape, mybir.dt.from_np(v.dtype), kind="ExternalInput").ap() for n, v in arrays.items()]
    args.append(nc.dram_tensor("outT", (D, 2, 4 * P), F32, kind="ExternalOutput").ap())
    build(nc, *args)
    r = run_bass_kernel_spmd(nc, [arrays], core_ids=[0])
    outT = r.results[0]["outT"]
    got = np.empty((NB, S, D), np.float32)
    for g, tiles in enumerate(GROUPS):
        for i, t in enumerate(tiles):
            at = i * P
            for b, p, n in TILES[t]:
                got[b, p:p + n] = outT[:, g, at:at + n].T
                at += n
    return got
```

```python
from contextlib import ExitStack

import numpy as np

import concourse.bass as bass
from concourse import mybir

F32 = mybir.dt.float32
F32R = mybir.dt.float32r
BF16 = mybir.dt.bfloat16
ALU = mybir.AluOpType
ACT = mybir.ActivationFunctionType
AX = mybir.AxisListType

P = 128
D = 128
NB = 2
S = 512
S_CTX = 77
WINDOW = 64
H = 16
DH = D // H
E = 8
F = 176
FS = 2 * F
HID = E * F + FS
NCH = -(-HID // P)
NEXP = E * F // P
NSH = NCH - NEXP
NARROW = FS - (NSH - 1) * P
assert NEXP * P == E * F
CW = 3 * P
GT = 4 * P
LN_EPS = 1e-5
TOP_SCALE = 2.5
TOP_EPS = 1e-20
MASKED = -1e30

TILES = [
    [(0, 0, 128)],
    [(1, 0, 128)],
    [(0, 128, 32), (1, 128, 32), (0, 160, 64)],
    [(0, 224, 128)],
    [(0, 352, 128)],
    [(0, 480, 32), (1, 160, 96)],
    [(1, 256, 128)],
    [(1, 384, 128)],
]
NT = len(TILES)
GROUPS = [[3, 4, 5, 6], [7, 0, 1, 2]]
ATT_ROWS = [128, 128, 64]
NQ = sum(ATT_ROWS)
QCOL = [0, 128, 256]
KEY2 = 128 - WINDOW
NK2 = S_CTX - KEY2
H2 = H // 2
R2 = H2 * NK2
STEPS = [(0, g) for g in range(4)] + [(1, g) for g in range(4)] + [(2, 0)]


def columns(**widths):
    at, found = 0, {}
    for name, w in widths.items():
        found[name] = (at, at + w)
        at += w
    return found, at


C1, C1_W = columns(ident=P, half=8, thr=E * E)
C2, C2_W = columns(cosk=NB * S_CTX, sink=NB * S_CTX, m4=4, m16=H, m8=H2, valid=1, cosq=NQ, sinq=NQ)
AW, AW_W = columns(ctxT=NB * S_CTX, kw=D, kws=D, vw=D, ctx2T=NB * R2, bias=4, gw=E, qw=D, qws=D, ow=D)
CB_W = P + S_CTX + NK2


def build(nc, x, attw, c1, c2, cbf, sel, rows, wall, out):
    with ExitStack() as ctx:
        def sb(name, shape, dt=F32):
            return ctx.enter_context(nc.sbuf_tensor(name, shape, dt))

        def sem(name):
            return ctx.enter_context(nc.semaphore(name))

        xr = sb("xr", [P, NT, D])
        attw_sb = sb("attw_sb", [P, AW_W])
        c1_sb = sb("c1_sb", [P, C1_W])
        c2_sb = sb("c2_sb", [P, C2_W])
        cb = sb("cb", [P, CB_W], BF16)
        ob = sb("ob", [P, D])
        vb = sb("vb", [P, D])
        sel_sb = sb("sel_sb", [2 * E, NEXP, P])
        sel_r = sb("sel_r", [2 * E, NEXP, P], F32R)
        w = sb("w", [P, NCH, CW])
        w_hi = sb("w_hi", [P, NCH, CW], F32R)
        w_lo = sb("w_lo", [P, NCH, CW], F32R)
        gw_hi = sb("gw_hi", [P, E], F32R)
        gw_lo = sb("gw_lo", [P, E], F32R)

        stats = sb("stats", [P, NT + 3, 6])
        mv = sb("mv", [P, NT + 3, 2])
        rstd = sb("rstd", [P, NT + 3])
        xn = sb("xn", [P, NT + 3, D])
        xn1T = sb("xn1T", [P, NQ])
        q1 = sb("q1", [P, NQ])
        q2 = sb("q2", [P, NQ])
        qT = sb("qT", [P, NQ])
        k1 = sb("k1", [P, NB * S_CTX])
        k2 = sb("k2", [P, NB * S_CTX])
        kT = sb("kT", [P, NB * S_CTX])
        kbd = sb("kbd", [P, NB, 4, S_CTX])
        kbd2 = sb("kbd2", [P, NB, H, NK2])
        vaug = sb("vaug", [S_CTX, NB, H, DH + 1])
        v2 = sb("v2", [R2, NB, D])
        vbd2 = sb("vbd2", [R2, NB, 2, H2, DH + 1])
        smax = sb("smax", [P, 8, 4])
        smax2 = sb("smax2", [64, H])
        prob = sb("prob", [P, 8, 4, S_CTX])
        prob2 = sb("prob2", [64, H, NK2])
        probT = sb("probT", [R2, 2, 4 * P])
        rden = sb("rden", [P, 3, H])
        cn = sb("cn", [P, 3, D])
        cT = sb("cT", [P, 3, P])

        lmax = sb("lmax", [P, 2, 4])
        lexp = sb("lexp", [P, 2, 4, E])
        lsum = sb("lsum", [P, 2, 4])
        lrec = sb("lrec", [P, 2, 4])
        lp = sb("lp", [P, 2, 4, E])
        ldif = sb("ldif", [P, 2, 4, E, E])
        lrank = sb("lrank", [P, 2, 4, E])
        lsel = sb("lsel", [P, 2, 4, E])
        tsum = sb("tsum", [P, 2, 4])
        trec = sb("trec", [P, 2, 4])
        comb = sb("comb", [P, 2, 4, E])
        comb2 = sb("comb2", [P, 2, 4, 2 * E])
        combT = sb("combT", [2 * E, 2, GT], F32R)
        spread = sb("spread", [P, NEXP, GT])

        xT_hi = sb("xT_hi", [P, 2, GT], F32R)
        xT_lo = sb("xT_lo", [P, 2, GT], F32R)
        xrT = sb("xrT", [P, 2, GT])
        sg = sb("sg", [P, 3, GT])
        sc = sb("sc", [P, 3, GT])
        hid = sb("hid", [P, 3, GT])
        hid_hi = sb("hid_hi", [P, 4, GT], F32R)
        hid_lo = sb("hid_lo", [P, 4, GT], F32R)
        y = sb("y", [P, 2, GT])

        bank = [ctx.enter_context(nc.psum_tensor(f"bank{i}", [P, 512], F32)) for i in range(8)]
        gate_ps, up_ps, down_ps, spread_ps = bank[0], bank[1:3], bank[3], (bank[4], bank[7])
        att = bank[5:8]
        scores_ps = att[0:2]
        pT_ps = [att[2], att[0]]
        ctx_ps = [att[1], bank[4], att[1]]
        TC, PC = 256, 384

        ld_xf, ld_xa, ld_x7 = sem("ld_xf"), sem("ld_xa"), sem("ld_x7")
        ld_attw, ld_c1, ld_c2, ld_cb = sem("ld_attw"), sem("ld_c1"), sem("ld_c2"), sem("ld_cb")
        ld_ob, ld_vb, ld_sel = sem("ld_ob"), sem("ld_vb"), sem("ld_sel")
        W_LOADS = [(0, 1), (1, 3), (3, 6), (6, 10), (10, NCH)]
        ld_w = [sem(f"ld_w{i}") for i in range(len(W_LOADS))]
        stored = sem("stored")
        dve_raw, pool_raw = sem("dve_raw"), sem("pool_raw")
        xr_ready = sem("xr_ready")
        var_ready, rstd_ready = sem("var_ready"), sem("rstd_ready")
        pool_gw, sel_ready, w_hi_ready = sem("pool_gw"), sem("sel_ready"), sem("w_hi_ready")
        w0_lo_ready, w_lo_ready = sem("w0_lo_ready"), sem("w_lo_ready")
        xn1_ready, xn1T_ps, xn1T_ready = sem("xn1_ready"), sem("xn1T_ps"), sem("xn1T_ready")
        k_ps, v_ps, q_ps = sem("k_ps"), sem("v_ps"), sem("q_ps")
        kT_ready, k2_ready, q_ready = sem("kT_ready"), sem("k2_ready"), sem("q_ready")
        v_ready, v2_ready = sem("v_ready"), sem("v2_ready")
        scores_done, scores_read, prob_ready = sem("scores_done"), sem("scores_read"), sem("prob_ready")
        pT_done, pT_read, ctx_done = sem("pT_done"), sem("pT_read"), sem("ctx_done")
        cn_ready, cT_ps, cT_ready = sem("cn_ready"), sem("cT_ps"), sem("cT_ready")
        o_ps, x1_ready = sem("o_ps"), sem("x1_ready")
        xn_ready = sem("xn_ready")
        xT_ps, xT_hi_ready, xT_lo_ready = sem("xT_ps"), sem("xT_hi_ready"), sem("xT_lo_ready")
        xrT_ps, xrT_ready = sem("xrT_ps"), sem("xrT_ready")
        logit_ps, logit_read, lexp_ready, comb_ready = sem("logit_ps"), sem("logit_read"), sem("lexp_ready"), sem("comb_ready")
        combT_ps, combT_ready, spread_done, spread_ready = (sem(n) for n in ("combT_ps", "combT_ready", "spread_done", "spread_ready"))
        gate_done, silu_done, scaled, up_done = sem("gate_done"), sem("silu_done"), sem("scaled"), sem("up_done")
        hid_done, hi_done, lo_done, down_done = sem("hid_done"), sem("hi_done"), sem("lo_done"), sem("down_done")
        y_ready = sem("y_ready")

        aw = {n: attw_sb[:, a:b] for n, (a, b) in AW.items()}
        cc = {n: c1_sb[:, a:b] for n, (a, b) in C1.items()} | {n: c2_sb[:, a:b] for n, (a, b) in C2.items()}
        ident = cc["ident"]
        identb, mask01, mask2 = cb[:, 0:P], cb[:, P:P + S_CTX], cb[:, P + S_CTX:CB_W]
        nk = NB * S_CTX

        def width(c):
            return NARROW if c == NSH - 1 else P

        def scaled_before(m):
            g, c = divmod(m, NCH)
            return g * NEXP + max(c - NSH, 0)

        def batches(t):
            return [(t, 0, P)] if t < 2 else [(0, 0, 32), (1, 32, 64)]

        block = ctx.enter_context(nc.Block())

        @block.sync
        def _(sp):
            sp.dma_start(xr[:, 3:7, :], x[:, 3:7, :]).then_inc(ld_xf, 16)
            sp.dma_start(c1_sb[:], c1).then_inc(ld_c1, 16)
            sp.dma_start(w[:, 0:1, :], wall[:, 0:1, :]).then_inc(ld_w[0], 16)
            sp.dma_start(c2_sb[:], c2).then_inc(ld_c2, 16)
            for i, (a, b) in list(enumerate(W_LOADS))[1:]:
                sp.dma_start(w[:, a:b, :], wall[:, a:b, :]).then_inc(ld_w[i], 16)
                if i == 1:
                    sp.dma_start(vb[:], rows[1:2, :].partition_broadcast(P)).then_inc(ld_vb, 16)
                if i == 2:
                    sp.dma_start(cb[:], cbf).then_inc(ld_cb, 16)
                if i == 3:
                    sp.dma_start(sel_sb[:], sel).then_inc(ld_sel, 16)
                    sp.dma_start(xr[:, 7:8, :], x[:, 7:8, :]).then_inc(ld_x7, 16)
            for g in range(2):
                for half in range(2):
                    sp.wait_ge(y_ready, 2 * g + half + 1)
                    cols = slice(256 * half, 256 * half + 256)
                    sp.dma_start(out[:, g, cols], y[:, g, cols]).then_inc(stored, 16)
            sp.wait_ge(stored, 16 * 4)

        @block.gpsimd
        def _(pool):
            n_raw, n_var = [0], [0]

            def then(ins):
                n_raw[0] += 1
                ins.then_inc(pool_raw, 1)
                pool.wait_ge(pool_raw, n_raw[0])

            def make_rstd(a, b):
                n_var[0] += 1
                pool.wait_ge(var_ready, n_var[0])
                then(nc.gpsimd.tensor_scalar(rstd[:, a:b], mv[:, a:b, 1], LN_EPS, None, ALU.add))
                nc.gpsimd.tensor_tensor(rstd[:, a:b], rstd[:, a:b], cc["half"][:, 0:b - a], ALU.pow).then_inc(rstd_ready, 1)

            def weights_low(c):
                pool.wait_ge(w_hi_ready, c + 1)
                nc.gpsimd.tensor_tensor(w_lo[:, c, :], w[:, c, :], w_hi[:, c, :].bitcast(F32), ALU.subtract).then_inc(w_lo_ready, 1)

            def block_last_keys():
                pool.wait_ge(kT_ready, 1)
                pool.wait_ge(v_ready, 1)
                for b in range(NB):
                    last = nc.gpsimd.tensor_tensor(
                        kbd2[:, b], kT[:, None, b * S_CTX + KEY2:(b + 1) * S_CTX].to_broadcast([P, H, NK2]),
                        cc["m16"][:, :, None].to_broadcast([P, H, NK2]), ALU.mult)
                last.then_inc(k2_ready, 1)
                m8 = cc["m8"][0:R2, None, :]
                bd = vbd2[:].rearrange("r b j h d -> r (b j) h d")
                nc.gpsimd.tensor_copy(bd[:, :, :, DH], m8.to_broadcast([R2, 2 * NB, H2]))
                nc.gpsimd.tensor_tensor(bd[:, :, :, 0:DH], v2[:].rearrange("r b (j h d) -> r (b j) h d", j=2, h=H2),
                                        m8[:, :, :, None].to_broadcast([R2, 2 * NB, H2, DH]), ALU.mult).then_inc(v2_ready, 1)

            pool.wait_ge(ld_c1, 16)
            make_rstd(3, 7)
            make_rstd(NT, NT + 3)
            pool.wait_ge(ld_attw, 16)
            then(nc.gpsimd.tensor_copy(gw_hi[:], aw["gw"]))
            nc.gpsimd.tensor_tensor(gw_lo[:], aw["gw"], gw_hi[:].bitcast(F32), ALU.subtract).then_inc(pool_gw, 1)
            for c in range(1, AHEAD):
                weights_low(c)
            for m in range(2 * NCH):
                c = m % NCH
                if c >= NSH:
                    pool.wait_ge(silu_done, m + 1)
                    pool.wait_ge(spread_ready, scaled_before(m) + 1)
                    if m >= 3:
                        pool.wait_ge(hid_done, m - 2)
                    nc.gpsimd.tensor_tensor(sc[:, m % 3, :], sg[:, m % 3, :], spread[:, c - NSH, :],
                                            ALU.mult).then_inc(scaled, 1)
                if m + AHEAD < NCH:
                    weights_low(m + AHEAD)
                if m == 4:
                    block_last_keys()
                if m == 6:
                    make_rstd(7, 8)
                for t in range(3):
                    if m == steps_at("project", t) // 2:
                        make_rstd(t, t + 1)

        @block.scalar
        def _(act):
            act.dma_start(ob[:], rows[0:1, :].partition_broadcast(P)).then_inc(ld_ob, 16)
            act.dma_start(xr[:, 0:3, :], x[:, 0:3, :]).then_inc(ld_xa, 16)
            act.dma_start(attw_sb[:], attw).then_inc(ld_attw, 16)

            def weights_high(c):
                if c in [a for a, _ in W_LOADS]:
                    act.wait_ge(ld_w[[a for a, _ in W_LOADS].index(c)], 16)
                nc.scalar.copy(w_hi[:, c, :], w[:, c, :]).then_inc(w_hi_ready, 1)

            def xT_high(g):
                act.wait_ge(xT_ps, g + 1)
                nc.scalar.copy(xT_hi[:, g, :], att[0][:, :]).then_inc(xT_hi_ready, 1)

            def xrT_copy(g):
                act.wait_ge(xrT_ps, g + 1)
                nc.scalar.copy(xrT[:, g, :], att[2][:, :]).then_inc(xrT_ready, 1)

            def route_exp(g):
                act.wait_ge(logit_read, g + 1)
                nc.scalar.activation(lexp[:, g], lexp[:, g], ACT.Exp).then_inc(lexp_ready, 1)

            def combT_copy(g):
                act.wait_ge(combT_ps, g + 1)
                nc.scalar.copy(combT[:, g, :], spread_ps[0][0:2 * E, :]).then_inc(combT_ready, 1)

            def spread_copy(n):
                act.wait_ge(spread_done, n + 1)
                if n >= NEXP:
                    act.wait_ge(scaled, n - NEXP + 1)
                nc.scalar.copy(spread[:, n % NEXP, :], spread_ps[n % NEXP % 2][:, :]).then_inc(spread_ready, 1)

            def attend_exp():
                for s in range(8):
                    act.wait_ge(scores_read, s + 1)
                    nc.scalar.activation(prob[:, s], prob[:, s], ACT.Exp).then_inc(prob_ready, 1)
                act.wait_ge(scores_read, 9)
                nc.scalar.activation(prob2[:], prob2[:], ACT.Exp).then_inc(prob_ready, 1)

            def silu(m):
                wc = width(m % NCH)
                act.wait_ge(gate_done, m + 1)
                if m >= 3:
                    act.wait_ge(hid_done, m - 2)
                nc.scalar.activation(sg[0:wc, m % 3, :], gate_ps[0:wc, :], ACT.Silu).then_inc(silu_done, 1)

            def hidden_high(m):
                wc = width(m % NCH)
                act.wait_ge(hid_done, m + 1)
                if m >= 4:
                    act.wait_ge(down_done, m - 3)
                nc.scalar.copy(hid_hi[0:wc, m % 4, :], hid[0:wc, m % 3, :]).then_inc(hi_done, 1)

            def ctxT_copy(t):
                r = ATT_ROWS[t]
                act.wait_ge(cT_ps, t + 1)
                nc.scalar.copy(cT[:, t, 0:r], ctx_ps[t][:, TC:TC + r]).then_inc(cT_ready, 1)

            weights_high(0)
            weights_high(1)
            xT_high(0)
            weights_high(2)
            act.wait_ge(xn1T_ps, 1)
            nc.scalar.copy(xn1T[:], down_ps[:, 0:NQ]).then_inc(xn1T_ready, 1)
            xrT_copy(0)
            for c in range(3, AHEAD):
                weights_high(c)
            route_exp(0)
            for m in range(2 * NCH):
                if m == EXP_UNIT:
                    attend_exp()
                if m == NCH:
                    route_exp(1)
                silu(m)
                if m == 2:
                    act.wait_ge(ld_sel, 16)
                    nc.scalar.copy(sel_r[:], sel_sb[:]).then_inc(sel_ready, 1)
                if m + AHEAD < NCH:
                    weights_high(m + AHEAD)
                for i in (2 * m, 2 * m + 1):
                    if i % (2 * NCH) == COMB_AT:
                        combT_copy(m // NCH)
                    spread_at(i, spread_copy)
                    for step, n in ATTENTION.get(i, []):
                        if step == "turn_ctx":
                            ctxT_copy(n)
                if m == NCH - 1:
                    xT_high(1)
                if m >= 1:
                    hidden_high(m - 1)
                if m == NCH - 1:
                    xrT_copy(1)
            hidden_high(2 * NCH - 1)

        @block.vector
        def _(dve):
            n_raw, n_rstd = [0], [0]

            def then(ins):
                n_raw[0] += 1
                ins.then_inc(dve_raw, 1)
                dve.wait_ge(dve_raw, n_raw[0])

            def norm_stats(tiles, at):
                for i, t in enumerate(tiles):
                    last = nc.vector.bn_stats(stats[:, at + i, :], xr[:, t, :])
                then(last)
                for i in range(len(tiles)):
                    last = nc.vector.bn_aggr(mv[:, at + i, :], stats[:, at + i, :])
                last.then_inc(var_ready, 1)

            def normalise(tiles, at):
                n_rstd[0] += 1
                dve.wait_ge(rstd_ready, n_rstd[0])
                for i, t in enumerate(tiles):
                    last = nc.vector.tensor_scalar(xn[:, at + i, :], xr[:, t, :], mv[:, at + i, 0:1],
                                                   rstd[:, at + i:at + i + 1], ALU.subtract, ALU.mult)
                return last

            def add_ob(a, b):
                return nc.vector.tensor_tensor(xr[:, a:b, :], xr[:, a:b, :],
                                               ob[:, None, :].to_broadcast([P, b - a, D]), ALU.add)

            def xT_low(g):
                dve.wait_ge(xT_hi_ready, g + 1)
                nc.vector.tensor_tensor(xT_lo[:, g, :], att[0][:, :], xT_hi[:, g, :].bitcast(F32),
                                        ALU.subtract).then_inc(xT_lo_ready, 1)

            def logit_bank(g):
                return (up_ps[1], att[1])[g][:, 0:4 * E]

            def route_sub(g):
                dve.wait_ge(logit_ps, g + 1)
                lg = logit_bank(g).rearrange("p (t e) -> p t e", t=4)
                then(nc.vector.tensor_reduce(lmax[:, g, :], lg, AX.X, ALU.max))
                nc.vector.tensor_tensor(lexp[:, g], lg, lmax[:, g, :, None].to_broadcast([P, 4, E]),
                                        ALU.subtract).then_inc(logit_read, 1)

            def route_probs(g):
                dve.wait_ge(lexp_ready, g + 1)
                then(nc.vector.tensor_reduce(lsum[:, g, :], lexp[:, g], AX.X, ALU.add))
                then(nc.vector.reciprocal(lrec[:, g, :], lsum[:, g, :]))
                then(nc.vector.tensor_tensor(lp[:, g], lexp[:, g], lrec[:, g, :, None].to_broadcast([P, 4, E]), ALU.mult))
                then(nc.vector.tensor_tensor(ldif[:, g], lp[:, g, :, None, :].to_broadcast([P, 4, E, E]),
                                             lp[:, g, :, :, None].to_broadcast([P, 4, E, E]), ALU.subtract))

            def route_rank(g):
                flat = ldif[:, g].rearrange("p t e j -> p t (e j)")
                then(nc.vector.tensor_tensor(flat, flat, cc["thr"][:, None, :].to_broadcast([P, 4, E * E]), ALU.is_ge))
                then(nc.vector.tensor_reduce(lrank[:, g], ldif[:, g], AX.X, ALU.add))
                then(nc.vector.scalar_tensor_tensor(out=lsel[:, g], in0=lrank[:, g], scalar=1.5, in1=lp[:, g],
                                                    op0=ALU.is_lt, op1=ALU.mult))
                then(nc.vector.tensor_reduce(tsum[:, g, :], lsel[:, g], AX.X, ALU.add))

            def route_weights(g):
                then(nc.vector.tensor_scalar(tsum[:, g, :], tsum[:, g, :], TOP_EPS, None, ALU.add))
                then(nc.vector.reciprocal(trec[:, g, :], tsum[:, g, :]))
                then(nc.vector.scalar_tensor_tensor(out=comb[:, g], in0=lsel[:, g], scalar=TOP_SCALE,
                                                    in1=trec[:, g, :, None].to_broadcast([P, 4, E]),
                                                    op0=ALU.mult, op1=ALU.mult))
                then(nc.vector.tensor_copy(comb2[:, g, :, 0:E].bitcast(F32R), comb[:, g]))
                nc.vector.tensor_tensor(comb2[:, g, :, E:2 * E], comb[:, g], comb2[:, g, :, 0:E],
                                        ALU.subtract).then_inc(comb_ready, 1)

            def rope(dst, a, b, in1, in2, bias1, bias2, cos, sin):
                nc.vector.scalar_tensor_tensor(out=a, in0=in1, scalar=bias1, in1=cos, op0=ALU.add, op1=ALU.mult)
                then(nc.vector.scalar_tensor_tensor(out=b, in0=in2, scalar=bias2, in1=sin, op0=ALU.add, op1=ALU.mult))
                return nc.vector.tensor_tensor(dst, a, b, ALU.add)

            def keys():
                dve.wait_ge(k_ps, 1)
                dve.wait_ge(ld_c2, 16)
                then(rope(kT[:], k1[:], k2[:], att[1][:, 0:nk], att[1][:, nk:2 * nk],
                          aw["bias"][:, 2:3], aw["bias"][:, 3:4], cc["cosk"], cc["sink"]))

            def block_keys():
                for b in range(NB):
                    last = nc.vector.tensor_tensor(kbd[:, b], kT[:, None, b * S_CTX:(b + 1) * S_CTX].to_broadcast([P, 4, S_CTX]),
                                                   cc["m4"][:, :, None].to_broadcast([P, 4, S_CTX]), ALU.mult)
                last.then_inc(kT_ready, 1)

            def values():
                dve.wait_ge(v_ps, 1)
                dve.wait_ge(ld_vb, 16)
                nc.vector.tensor_tensor(v2[:], spread_ps[0][0:R2, NB * D:2 * NB * D].rearrange("k (b d) -> k b d", b=NB),
                                        vb[0:R2, None, :].to_broadcast([R2, NB, D]), ALU.add)
                for b in range(NB):
                    last = nc.vector.tensor_tensor(
                        vaug[:, b, :, 0:DH],
                        spread_ps[0][0:S_CTX, b * D:(b + 1) * D].rearrange("k (h d) -> k h d", h=H),
                        vb[0:S_CTX, :].rearrange("k (h d) -> k h d", h=H), ALU.add)
                last.then_inc(v_ready, 1)

            def softmax_max(s):
                dve.wait_ge(scores_done, s + 1)
                if s < 8:
                    sc_ = scores_ps[s % 2][:, 0:4 * S_CTX].rearrange("q (h k) -> q h k", h=4)
                    top, dst, shape = smax[:, s, :], prob[:, s], [P, 4, S_CTX]
                else:
                    sc_ = scores_ps[s % 2][0:64, 0:H * NK2].rearrange("q (h k) -> q h k", h=H)
                    top, dst, shape = smax2[:], prob2[:], [64, H, NK2]
                then(nc.vector.tensor_reduce(top, sc_, AX.X, ALU.max))
                nc.vector.tensor_tensor(dst, sc_, top[:, :, None].to_broadcast(shape), ALU.subtract).then_inc(scores_read, 1)

            def probT_copy(p):
                dve.wait_ge(pT_done, p + 1)
                if p >= 2:
                    dve.wait_ge(ctx_done, p - 1)
                r, n = (S_CTX, 4 * P) if p < 8 else (R2, 2 * 64)
                nc.vector.tensor_copy(probT[0:r, p % 2, 0:n], pT_ps[p % 2][0:r, 0:n]).then_inc(pT_read, 1)

            def ctx_norm(t):
                r = ATT_ROWS[t]
                dve.wait_ge(ctx_done, (4, 8, 9)[t])
                cv = ctx_ps[t][0:r, 0:H * (DH + 1)].rearrange("q (h d) -> q h d", h=H)
                then(nc.vector.reciprocal(rden[0:r, t, :], cv[:, :, DH]))
                nc.vector.tensor_tensor(cn[0:r, t, :].rearrange("q (h d) -> q h d", h=H), cv[:, :, 0:DH],
                                        rden[0:r, t, :, None].to_broadcast([r, H, DH]), ALU.mult).then_inc(cn_ready, 1)

            def add_attention(t):
                r = ATT_ROWS[t]
                dve.wait_ge(o_ps, t + 1)
                scalar = 1.0 if t < 2 else cc["valid"][0:r, :]
                ins = nc.vector.scalar_tensor_tensor(out=xr[0:r, t, :], in0=ctx_ps[t][0:r, PC:PC + D], scalar=scalar,
                                                     in1=xr[0:r, t, :], op0=ALU.mult, op1=ALU.add)
                ins.then_inc(x1_ready, 1)
                dve.wait_ge(x1_ready, t + 1)
                norm_stats([t], t)

            def hidden(m):
                g, c = divmod(m, NCH)
                wc = width(c)
                if c >= NSH:
                    dve.wait_ge(scaled, scaled_before(m) + 1)
                else:
                    dve.wait_ge(silu_done, m + 1)
                dve.wait_ge(up_done, m + 1)
                if m >= 3:
                    dve.wait_ge(hi_done, m - 2)
                    dve.wait_ge(lo_done, m - 2)
                s = (sc if c >= NSH else sg)[0:wc, m % 3, :]
                nc.vector.tensor_tensor(hid[0:wc, m % 3, :], s, up_ps[m % 2][0:wc, :], ALU.mult).then_inc(hid_done, 1)

            def hidden_low(m):
                wc = width(m % NCH)
                dve.wait_ge(hi_done, m + 1)
                if m >= 4:
                    dve.wait_ge(down_done, m - 3)
                nc.vector.tensor_tensor(hid_lo[0:wc, m % 4, :], hid[0:wc, m % 3, :],
                                        hid_hi[0:wc, m % 4, :].bitcast(F32), ALU.subtract).then_inc(lo_done, 1)

            def finish(g):
                dve.wait_ge(down_done, NCH * (g + 1))
                dve.wait_ge(xrT_ready, g + 1)
                for half in range(2):
                    cols = slice(256 * half, 256 * half + 256)
                    nc.vector.tensor_tensor(y[:, g, cols], down_ps[:, cols], xrT[:, g, cols], ALU.add).then_inc(y_ready, 1)

            nc.vector.memset(vaug[:], 1.0)
            dve.wait_ge(ld_xf, 16)
            dve.wait_ge(ld_ob, 16)
            then(add_ob(3, 7))
            norm_stats([3, 4, 5, 6], 3)
            dve.wait_ge(ld_xa, 16)
            norm_stats([0, 1, 2], NT)
            normalise([3, 4, 5, 6], 3).then_inc(xn_ready, 1)
            dve.wait_ge(w_hi_ready, 1)
            nc.vector.tensor_tensor(w_lo[:, 0, :], w[:, 0, :], w_hi[:, 0, :].bitcast(F32),
                                    ALU.subtract).then_inc(w0_lo_ready, 1)
            normalise([0, 1, 2], NT).then_inc(xn1_ready, 1)
            xT_low(0)
            dve.wait_ge(xn1_ready, 1)
            add_ob(0, 3)
            keys()
            values()
            route_sub(0)
            block_keys()
            dve.wait_ge(q_ps, 1)
            rope(qT[:], q1[:], q2[:], down_ps[:, 0:NQ], att[0][:, 0:NQ],
                 aw["bias"][:, 0:1], aw["bias"][:, 1:2], cc["cosq"], cc["sinq"]).then_inc(q_ready, 1)

            for m in range(2 * NCH):
                g, c = divmod(m, NCH)
                if m == NCH - 1:
                    xT_low(1)
                if m == NCH:
                    route_sub(1)
                    route_probs(1)
                    route_rank(1)
                if m == NCH + 2:
                    finish(0)
                for i in (2 * m, 2 * m + 1):
                    for step, n in ATTENTION.get(i - 2, []):
                        if step == "project":
                            normalise([n], n).then_inc(xn_ready, 1)
                    for step, n in ATTENTION.get(i, []):
                        if step == "scores":
                            softmax_max(n)
                        if step == "turn_probs":
                            probT_copy(n)
                        if step == "context" and n in (3, 7, 8):
                            ctx_norm(min(n // 4, 2))
                        if step == "project":
                            add_attention(n)
                if m == 7:
                    normalise([7], 7).then_inc(xn_ready, 1)
                hidden(m)
                if m >= 1:
                    hidden_low(m - 1)
                if m == 0:
                    route_probs(0)
                if m == 1:
                    route_rank(0)
                if m in (2, NCH):
                    route_weights(g)
                if m == 5:
                    dve.wait_ge(ld_x7, 16)
                    then(add_ob(7, 8))
                    norm_stats([7], 7)
            hidden_low(2 * NCH - 1)
            finish(1)

        @block.tensor
        def _(pe):
            def turn_x(g):
                for i, t in enumerate(GROUPS[g]):
                    last = nc.tensor.transpose(att[0][:, i * P:(i + 1) * P], xn[:, t, :], ident)
                last.then_inc(xT_ps, 1)

            def turn_xr(g):
                for i, t in enumerate(GROUPS[g]):
                    last = nc.tensor.transpose(att[2][:, i * P:(i + 1) * P], xr[:, t, :], ident)
                last.then_inc(xrT_ps, 1)

            def logits(g):
                bl = (up_ps[1], att[1])[g]
                pe.wait_ge(xT_lo_ready, g + 1)
                for i in range(4):
                    o, c = bl[:, i * E:(i + 1) * E], slice(i * P, (i + 1) * P)
                    nc.tensor.matmul(o, xT_hi[:, g, c], gw_hi[:], start=True, stop=False)
                    nc.tensor.matmul(o, xT_hi[:, g, c], gw_lo[:], start=False, stop=False)
                    last = nc.tensor.matmul(o, xT_lo[:, g, c], gw_hi[:], start=False, stop=True)
                last.then_inc(logit_ps, 1)

            def turn_comb(g):
                pe.wait_ge(comb_ready, g + 1)
                if g == 0:
                    pe.wait_ge(v_ready, 1)
                for i in range(4):
                    last = nc.tensor.transpose(spread_ps[0][0:2 * E, i * P:(i + 1) * P], comb2[:, g, i, :], ident)
                last.then_inc(combT_ps, 1)

            def spread_comb(n):
                g, c = divmod(n, NEXP)
                if c == 0:
                    pe.wait_ge(combT_ready, g + 1)
                    pe.wait_ge(xrT_ready, g + 1)
                if c >= 2:
                    pe.wait_ge(spread_ready, n - 1)
                nc.tensor.matmul(spread_ps[c % 2][:, :], sel_r[:, c, :], combT[:, g, :], start=True, stop=True).then_inc(spread_done, 1)

            def product(dst, c, cols, g, done):
                wh, wl = w_hi[:, c, cols], w_lo[:, c, cols]
                nc.tensor.matmul(dst, wh, xT_hi[:, g, :], start=True, stop=False)
                nc.tensor.matmul(dst, wh, xT_lo[:, g, :], start=False, stop=False)
                nc.tensor.matmul(dst, wl, xT_hi[:, g, :], start=False, stop=True).then_inc(done, 1)

            def gate(m):
                g, c = divmod(m, NCH)
                wc = width(c)
                if m == 0:
                    pe.wait_ge(w0_lo_ready, 1)
                elif g == 0:
                    pe.wait_ge(w_lo_ready, c)
                if c == 0:
                    pe.wait_ge(xT_lo_ready, g + 1)
                if m >= 1:
                    pe.wait_ge(silu_done, m)
                product(gate_ps[0:wc, :], c, slice(0, wc), g, gate_done)

            def up(m):
                g, c = divmod(m, NCH)
                wc = width(c)
                if m == 1:
                    pe.wait_ge(logit_read, 1)
                if m >= 2:
                    pe.wait_ge(hid_done, m - 1)
                product(up_ps[m % 2][0:wc, :], c, slice(P, P + wc), g, up_done)

            def down(m):
                g, c = divmod(m, NCH)
                wc = width(c)
                wh, wl = w_hi[0:wc, c, 2 * P:3 * P], w_lo[0:wc, c, 2 * P:3 * P]
                hh, hl = hid_hi[0:wc, m % 4, :], hid_lo[0:wc, m % 4, :]
                if m == 0:
                    pe.wait_ge(q_ready, 1)
                if m == NCH:
                    pe.wait_ge(y_ready, 2)
                pe.wait_ge(hi_done, m + 1)
                nc.tensor.matmul(down_ps[:, :], wh, hh, start=(c == 0), stop=False)
                nc.tensor.matmul(down_ps[:, :], wl, hh, start=False, stop=False)
                pe.wait_ge(lo_done, m + 1)
                nc.tensor.matmul(down_ps[:, :], wh, hl, start=False, stop=(c == NCH - 1)).then_inc(down_done, 1)

            def scores(s):
                t, g = STEPS[s]
                dst = scores_ps[s % 2]
                if s == 0:
                    pe.wait_ge(ld_cb, 16)
                    pe.wait_ge(kT_ready, 1)
                    pe.wait_ge(q_ready, 1)
                if s == 8:
                    pe.wait_ge(k2_ready, 1)
                if s >= 2:
                    pe.wait_ge(scores_read, s - 1)
                if t < 2:
                    nc.tensor.matmul(dst[:, 0:4 * S_CTX], identb, mask01[:, None, :].to_broadcast([P, 4, S_CTX]),
                                     start=True, stop=False, skip_group_check=True)
                    r = slice(32 * g, 32 * g + 32)
                    nc.tensor.matmul(dst[:, 0:4 * S_CTX], qT[r, QCOL[t]:QCOL[t] + P], kbd[r, t].rearrange("p h k -> p (h k)"),
                                     start=False, stop=True, skip_group_check=True).then_inc(scores_done, 1)
                    return
                nc.tensor.matmul(dst[0:64, 0:H * NK2], identb[0:64, 0:64], mask2[0:64, None, :].to_broadcast([64, H, NK2]),
                                 start=True, stop=False, skip_group_check=True)
                for b, q0, q1_ in batches(t):
                    last = nc.tensor.matmul(dst[q0:q1_, 0:H * NK2], qT[:, QCOL[t] + q0:QCOL[t] + q1_],
                                            kbd2[:, b].rearrange("p h k -> p (h k)"), start=False, stop=True,
                                            skip_group_check=True)
                last.then_inc(scores_done, 1)

            def turn_probs(p):
                pe.wait_ge(prob_ready, p + 1 if p < 8 else 9)
                if p == 0:
                    pe.wait_ge(scores_read, 9)
                    pe.wait_ge(spread_ready, NEXP)
                if p >= 2:
                    pe.wait_ge(pT_read, p - 1)
                if p < 8:
                    for hh in range(4):
                        last = nc.tensor.transpose(pT_ps[p % 2][0:S_CTX, hh * P:(hh + 1) * P], prob[:, p, hh, :], ident)
                else:
                    for j in range(2):
                        last = nc.tensor.transpose(pT_ps[p % 2][0:R2, j * 64:(j + 1) * 64],
                                                   prob2[:, j * H2:(j + 1) * H2, :].rearrange("q h k -> q (h k)"), ident[0:64, 0:64])
                last.then_inc(pT_done, 1)

            def context(p):
                t = min(p // 4, 2)
                pe.wait_ge(pT_read, p + 1)
                if p == 8:
                    pe.wait_ge(x1_ready, 1)
                    pe.wait_ge(v2_ready, 1)
                    for b, q0, q1_ in batches(t):
                        for j in range(2):
                            w_ = H2 * (DH + 1)
                            last = nc.tensor.matmul(ctx_ps[t][q0:q1_, j * w_:(j + 1) * w_],
                                                    probT[0:R2, p % 2, j * 64 + q0:j * 64 + q1_],
                                                    vbd2[:, b, j].rearrange("r h d -> r (h d)"), start=True, stop=True)
                else:
                    for hh in range(4):
                        h = 4 * (p % 4) + hh
                        last = nc.tensor.matmul(ctx_ps[t][:, h * (DH + 1):(h + 1) * (DH + 1)],
                                                probT[0:S_CTX, p % 2, hh * P:(hh + 1) * P], vaug[:, t, h, :],
                                                start=True, stop=True)
                last.then_inc(ctx_done, 1)

            def turn_ctx(t):
                r = ATT_ROWS[t]
                pe.wait_ge(cn_ready, t + 1)
                nc.tensor.transpose(ctx_ps[t][:, TC:TC + r], cn[0:r, t, :], ident[0:r, 0:r]).then_inc(cT_ps, 1)

            def project_out(t):
                r = ATT_ROWS[t]
                pe.wait_ge(cT_ready, t + 1)
                nc.tensor.matmul(ctx_ps[t][0:r, PC:PC + D], cT[:, t, 0:r], aw["ow"], start=True, stop=True).then_inc(o_ps, 1)

            pe.wait_ge(ld_attw, 16)
            nc.tensor.matmul(att[1][:, 0:nk], aw["kw"], aw["ctxT"], start=True, stop=True)
            nc.tensor.matmul(att[1][:, nk:2 * nk], aw["kws"], aw["ctxT"], start=True, stop=True).then_inc(k_ps, 1)
            pe.wait_ge(ld_c1, 16)
            pe.wait_ge(xn_ready, 1)
            turn_x(0)
            for keys_T, r, at in (("ctxT", S_CTX, 0), ("ctx2T", R2, NB * D)):
                for b in range(NB):
                    last = nc.tensor.matmul(spread_ps[0][0:r, at + b * D:at + (b + 1) * D],
                                            aw[keys_T][:, b * r:(b + 1) * r], aw["vw"], start=True, stop=True)
            last.then_inc(v_ps, 1)
            pe.wait_ge(xn1_ready, 1)
            for t in range(3):
                r = ATT_ROWS[t]
                last = nc.tensor.transpose(down_ps[:, QCOL[t]:QCOL[t] + r], xn[0:r, NT + t, :], ident[0:r, 0:r])
            last.then_inc(xn1T_ps, 1)
            turn_xr(0)
            for m in range(2 * NCH):
                g, c = divmod(m, NCH)
                for i in (2 * m, 2 * m + 1):
                    if i == 0:
                        pe.wait_ge(pool_gw, 1)
                        logits(0)
                    if i % 2 == 0:
                        gate(m)
                    else:
                        up(m)
                    if i == 1:
                        pe.wait_ge(xn1T_ready, 1)
                        nc.tensor.matmul(down_ps[:, 0:NQ], aw["qw"], xn1T[:], start=True, stop=True)
                        nc.tensor.matmul(att[0][:, 0:NQ], aw["qws"], xn1T[:], start=True, stop=True).then_inc(q_ps, 1)
                    if i == 2 * NCH - 2:
                        pe.wait_ge(xn_ready, 5)
                        turn_x(1)
                    if i == 8:
                        pe.wait_ge(sel_ready, 1)
                    spread_at(i, spread_comb)
                    for step, n in ATTENTION.get(i, []):
                        {"scores": scores, "turn_probs": turn_probs, "context": context,
                         "turn_ctx": turn_ctx, "project": project_out}[step](n)
                    if i % (2 * NCH) == COMB_AT:
                        turn_comb(g)
                for n in {NCH - 1: [m - 3, m - 2], NCH: [m - 2], NCH + 1: [m - 2], NCH + 2: [],
                          2 * NCH - 1: [m - 3, m - 2, m - 1, m]}.get(m, [m - 3]):
                    if n >= 0:
                        down(n)
                    if n == NCH - 4:
                        turn_xr(1)
                    if n == NCH - 3:
                        logits(1)


AHEAD = 5
COMB_AT = 7
SPREAD_AT = [[8, 8, 9, 9, 10, 10, 11, 11, 12, 12, 13],
             [8, 8, 9, 10, 11, 12, 13, 14, 15, 16, 17]]
EXP_UNIT = 7
SCORES_AT = [6, 7, 8, 9, 10, 11, 12, 13, 13]
ATTENTION = {i: [("scores", n) for n in range(9) if SCORES_AT[n] == i] for i in SCORES_AT} | {
    14: [("turn_probs", 0), ("turn_probs", 1), ("context", 0), ("turn_probs", 2), ("context", 1)],
    15: [("turn_probs", 3), ("context", 2)],
    16: [("turn_probs", 4), ("context", 3)],
    17: [("turn_probs", 5), ("context", 4)],
    18: [("turn_probs", 6), ("context", 5), ("turn_ctx", 0)],
    19: [("turn_probs", 7), ("context", 6), ("project", 0)],
    20: [("turn_probs", 8), ("context", 7)],
    21: [("context", 8), ("turn_ctx", 1)],
    22: [("project", 1), ("turn_ctx", 2)],
    23: [("project", 2)],
}


def steps_at(step, n):
    return [i for i, steps in ATTENTION.items() if (step, n) in steps][0]


def spread_at(i, spread_one):
    g, j = divmod(i, 2 * NCH)
    for e, at in enumerate(SPREAD_AT[g]):
        if at == j:
            spread_one(g * NEXP + e)


def positions(tile):
    return np.concatenate([np.arange(p, p + n) for _, p, n in TILES[tile]])


def rope_tables(pos, scale):
    half = DH // 2
    freqs = np.float32(1.0) / np.float32(10000.0) ** (np.arange(half, dtype=np.float32) / np.float32(half))
    ang = pos.astype(np.float32)[None, :] * freqs[:, None]
    cos, sin = np.cos(ang), np.sin(ang)
    cos = np.tile(np.concatenate([cos, cos]), (H, 1)) * scale
    sin = np.tile(np.concatenate([-sin, sin]), (H, 1)) * scale
    return cos.astype(np.float32), sin.astype(np.float32)


def constants():
    c1 = np.zeros((P, C1_W), np.float32)
    c2 = np.zeros((P, C2_W), np.float32)

    def put(name, value):
        dst, where = (c1, C1) if name in C1 else (c2, C2)
        a, b = where[name]
        dst[:, a:b] = value

    put("ident", np.eye(P))
    put("half", -0.5)
    e, j = np.meshgrid(np.arange(E), np.arange(E), indexing="ij")
    tiny = np.finfo(np.float32).tiny
    put("thr", np.where(j < e, 0.0, np.where(j > e, tiny, 2.0)).reshape(1, E * E))
    cos, sin = rope_tables(np.tile(np.arange(S_CTX), NB), 1.0)
    put("cosk", cos)
    put("sink", sin)
    cos, sin = rope_tables(np.concatenate([positions(t)[0:ATT_ROWS[t]] for t in range(3)]), DH ** -0.5)
    put("cosq", cos)
    put("sinq", sin)
    rows = np.arange(P)
    put("m4", (rows % 32 // DH)[:, None] == np.arange(4)[None, :])
    put("m16", (rows // DH)[:, None] == np.arange(H)[None, :])
    valid = np.zeros(P)
    valid[0:64] = positions(2)[0:64] - WINDOW < S_CTX
    put("valid", valid[:, None])
    put("m8", (rows // NK2)[:, None] == np.arange(H2)[None, :])

    def mask(pos, keys):
        return np.where((keys[None, :] <= pos[:, None]) & (keys[None, :] >= pos[:, None] - WINDOW), 0.0, MASKED)

    cbf = np.zeros((P, CB_W), np.float32)
    cbf[:, 0:P] = np.eye(P)
    cbf[:, P:P + S_CTX] = mask(positions(0), np.arange(S_CTX))
    cbf[:, P + S_CTX:] = mask(positions(2), np.arange(KEY2, S_CTX))
    feature = np.arange(NEXP * P).reshape(NEXP, P)
    sel = (np.tile(np.arange(E), 2)[:, None, None] == feature[None] // F).astype(np.float32)
    return c1, c2, cbf, sel


def kernel(**inputs):
    import ml_dtypes
    import concourse.bacc as bacc
    from concourse.bass_utils import run_bass_kernel_spmd

    a = {n: np.asarray(v) for n, v in inputs.items()}
    x = a["x"]
    xt = np.stack([np.concatenate([x[b, p:p + n] for b, p, n in runs]) for runs in TILES], axis=1)
    swap = np.arange(D).reshape(H, 2, DH // 2)[:, ::-1].reshape(D)
    ctx2 = np.repeat(a["ctx_1024"][:, None, KEY2:, :], H2, axis=1)
    att = {
        "ctxT": a["ctx_1024"].reshape(NB * S_CTX, D).T,
        "ctx2T": ctx2.reshape(NB * R2, D).T,
        "kw": a["L0_xattn_k_w"].T, "kws": a["L0_xattn_k_w"][swap].T, "vw": a["L0_xattn_v_w"].T,
        "qw": a["L0_xattn_q_w"].T, "qws": a["L0_xattn_q_w"][swap].T, "ow": a["L0_xattn_o_w"].T,
        "bias": np.stack([a["L0_xattn_q_b"], a["L0_xattn_q_b"][swap], a["L0_xattn_k_b"], a["L0_xattn_k_b"][swap]], axis=1),
        "gw": a["L0_ffn_gate_w"].T,
    }
    attw = np.concatenate([att[n] for n in AW], axis=1)

    def features(experts, shared):
        flat = np.concatenate([shared, np.zeros((D, NCH * P - HID), np.float32), experts.transpose(1, 0, 2).reshape(D, E * F)], axis=1)
        return flat.reshape(D, NCH, P)

    down = np.concatenate([a["L0_ffn_sw_down"], np.zeros((NCH * P - HID, D), np.float32),
                           a["L0_ffn_w_down"].reshape(E * F, D)])
    wall = np.concatenate([features(a["L0_ffn_w_gate"], a["L0_ffn_sw_gate"]), features(a["L0_ffn_w_up"], a["L0_ffn_sw_up"]),
                           down.reshape(NCH, P, D).transpose(1, 0, 2)], axis=2)
    rows = np.stack([a["L0_xattn_o_b"], a["L0_xattn_v_b"]])
    c1, c2, cbf, sel = constants()
    arrays = {"x_tiles": xt, "attw": attw, "c1": c1, "c2": c2, "cbf": cbf.astype(ml_dtypes.bfloat16), "sel": sel,
              "rows": rows, "wall": wall}
    arrays = {n: np.ascontiguousarray(v) for n, v in arrays.items()}

    nc = bacc.Bacc("TRN2", target_bir_lowering=False, num_devices=1)
    args = [nc.dram_tensor(n, v.shape, mybir.dt.from_np(v.dtype), kind="ExternalInput").ap() for n, v in arrays.items()]
    args.append(nc.dram_tensor("outT", (D, 2, 4 * P), F32, kind="ExternalOutput").ap())
    build(nc, *args)
    r = run_bass_kernel_spmd(nc, [arrays], core_ids=[0])
    outT = r.results[0]["outT"]
    got = np.empty((NB, S, D), np.float32)
    for g, tiles in enumerate(GROUPS):
        for i, t in enumerate(tiles):
            at = i * P
            for b, p, n in TILES[t]:
                got[b, p:p + n] = outT[:, g, at:at + n].T
                at += n
    return got
```

```python
from contextlib import ExitStack

import numpy as np

import concourse.bass as bass
from concourse import mybir

F32 = mybir.dt.float32
F32R = mybir.dt.float32r
BF16 = mybir.dt.bfloat16
ALU = mybir.AluOpType
ACT = mybir.ActivationFunctionType
AX = mybir.AxisListType

P = 128
D = 128
NB = 2
S = 512
S_CTX = 77
WINDOW = 64
H = 16
DH = D // H
E = 8
F = 176
FS = 2 * F
HID = E * F + FS
NCH = -(-HID // P)
NEXP = E * F // P
NSH = NCH - NEXP
NARROW = FS - (NSH - 1) * P
assert NEXP * P == E * F
CW = 3 * P
GT = 4 * P
HALVES = [slice(0, GT // 2), slice(GT // 2, GT)]
LAST = 2 * NCH - 1
POOL_LOW = [NCH - 1, LAST - 1]
LN_EPS = 1e-5
TOP_SCALE = 2.5
TOP_EPS = 1e-20
MASKED = -1e30

TILES = [
    [(0, 0, 128)],
    [(1, 0, 128)],
    [(0, 128, 32), (1, 128, 32), (0, 160, 64)],
    [(0, 224, 128)],
    [(0, 352, 128)],
    [(0, 480, 32), (1, 160, 96)],
    [(1, 256, 128)],
    [(1, 384, 128)],
]
NT = len(TILES)
GROUPS = [[3, 4, 5, 6], [7, 0, 1, 2]]
ATT_ROWS = [128, 128, 64]
NQ = sum(ATT_ROWS)
QCOL = [0, 128, 256]
KEY2 = 128 - WINDOW
NK2 = S_CTX - KEY2
H2 = H // 2
R2 = H2 * NK2
STEPS = [(0, g) for g in range(4)] + [(1, g) for g in range(4)] + [(2, 0)]


def columns(**widths):
    at, found = 0, {}
    for name, w in widths.items():
        found[name] = (at, at + w)
        at += w
    return found, at


C1, C1_W = columns(ident=P, half=8, thr=E * E)
C2, C2_W = columns(cosk=NB * S_CTX, sink=NB * S_CTX, m16=H, m8=H2, valid=1, cosq=NQ, sinq=NQ)
AW, AW_W = columns(ctxT=NB * S_CTX, kw=D, kws=D, vw=D, ctx2T=NB * R2, bias=4, gw=E, qw=D, qws=D, ow=D)
CB_W = P + S_CTX + NK2


def build(nc, x, attw, c1, c2, cbf, sel, rows, wall, out):
    with ExitStack() as ctx:
        def sb(name, shape, dt=F32):
            return ctx.enter_context(nc.sbuf_tensor(name, shape, dt))

        def sem(name):
            return ctx.enter_context(nc.semaphore(name))

        xr = sb("xr", [P, NT, D])
        attw_sb = sb("attw_sb", [P, AW_W])
        c1_sb = sb("c1_sb", [P, C1_W])
        c2_sb = sb("c2_sb", [P, C2_W])
        cb = sb("cb", [P, CB_W], BF16)
        ob = sb("ob", [P, D])
        vb = sb("vb", [P, D])
        sel_sb = sb("sel_sb", [2 * E, NEXP, P])
        sel_r = sb("sel_r", [2 * E, NEXP, P], F32R)
        w = sb("w", [P, NCH, CW])
        w_hi = sb("w_hi", [P, NCH, CW], F32R)
        w_lo = sb("w_lo", [P, NCH, CW], F32R)
        gw_hl = sb("gw_hl", [P, 2 * E], F32R)

        stats = sb("stats", [P, NT + 3, 6])
        mv = sb("mv", [P, NT + 3, 2])
        rstd = sb("rstd", [P, NT + 3])
        xn = sb("xn", [P, NT + 3, D])
        xn1T = sb("xn1T", [P, NQ])
        q2 = sb("q2", [P, NQ])
        qT = sb("qT", [P, NQ])
        k2 = sb("k2", [P, NB * S_CTX])
        kT = sb("kT", [P, NB * S_CTX])
        kbd = sb("kbd", [P, NB, H, S_CTX])
        vaug = sb("vaug", [S_CTX, NB, H, DH + 1])
        v2 = sb("v2", [R2, NB, D])
        vbd2 = sb("vbd2", [R2, NB, 2, H2, DH + 1])
        smax = sb("smax", [P, 8, 4])
        smax2 = sb("smax2", [64, H])
        prob = sb("prob", [P, 8, 4, S_CTX])
        prob2 = sb("prob2", [64, H, NK2])
        probT = sb("probT", [R2, 2, 4 * P])
        rden = sb("rden", [P, 3, H])
        cn = sb("cn", [P, 3, D])
        cT = sb("cT", [P, 3, P])

        lg = sb("lg", [P, 2, 4, E])
        lmax = sb("lmax", [P, 2, 4])
        lexp = sb("lexp", [P, 2, 4, E])
        lsum = sb("lsum", [P, 2, 4])
        lrec = sb("lrec", [P, 2, 4])
        lp = sb("lp", [P, 2, 4, E])
        ldif = sb("ldif", [P, 2, 4, E, E])
        lrank = sb("lrank", [P, 2, 4, E])
        lsel = sb("lsel", [P, 2, 4, E])
        tsum = sb("tsum", [P, 2, 4])
        trec = sb("trec", [P, 2, 4])
        comb = sb("comb", [P, 2, 4, E])
        comb2 = sb("comb2", [P, 2, 4, 2 * E])
        combT = sb("combT", [2 * E, 2, GT], F32R)
        spread = sb("spread", [P, NEXP, GT])

        xT_hi = sb("xT_hi", [P, 2, GT], F32R)
        xT_lo = sb("xT_lo", [P, 2, GT], F32R)
        xrT = sb("xrT", [P, 2, GT])
        sg = sb("sg", [P, 3, GT])
        sc = sb("sc", [P, 3, GT])
        hid = sb("hid", [P, 3, GT])
        hid_hi = sb("hid_hi", [P, 4, GT], F32R)
        hid_lo = sb("hid_lo", [P, 4, GT], F32R)
        last_hid_hi, last_hid_lo = xT_hi[:, 0, :], xT_lo[:, 0, :]

        bank = [ctx.enter_context(nc.psum_tensor(f"bank{i}", [P, 512], F32)) for i in range(8)]
        gate_ps, up_ps, down_ps = bank[0], bank[1:3], bank[3]
        spread_ps = (bank[4], bank[7])
        att = bank[5:8]
        scores_ps = att[0:2]
        pT_ps = [att[2], att[0]]
        ctx_ps = [att[1], bank[4], att[1]]
        TC, PC = 256, 384

        ld_xf, ld_xa, ld_x7 = sem("ld_xf"), sem("ld_xa"), sem("ld_x7")
        ld_attw, ld_c1, ld_c2, ld_cb = sem("ld_attw"), sem("ld_c1"), sem("ld_c2"), sem("ld_cb")
        ld_ob, ld_vb, ld_sel = sem("ld_ob"), sem("ld_vb"), sem("ld_sel")
        W_LOADS = [(0, 1), (1, 3), (3, 6), (6, 10), (10, NCH)]
        ld_w = [sem(f"ld_w{i}") for i in range(len(W_LOADS))]
        stored = sem("stored")
        dve_raw, pool_raw = sem("dve_raw"), sem("pool_raw")
        pool_added = sem("pool_added")
        var_ready, rstd_ready = sem("var_ready"), sem("rstd_ready")
        pool_gw, sel_ready, w_hi_ready = sem("pool_gw"), sem("sel_ready"), sem("w_hi_ready")
        w0_lo_ready, w_lo_ready = sem("w0_lo_ready"), sem("w_lo_ready")
        xn1_ready, xn1T_ps, xn1T_ready = sem("xn1_ready"), sem("xn1T_ps"), sem("xn1T_ready")
        k_ps, v_ps, q_ps = sem("k_ps"), sem("v_ps"), sem("q_ps")
        kT_ready, q_ready = sem("kT_ready"), sem("q_ready")
        kbd_ready = sem("kbd_ready")
        v_ready, v2_ready = sem("v_ready"), sem("v2_ready")
        scores_done, scores_read, prob_ready = sem("scores_done"), sem("scores_read"), sem("prob_ready")
        pT_done, pT_read, ctx_done = sem("pT_done"), sem("pT_read"), sem("ctx_done")
        cn_ready, cT_ps, cT_ready = sem("cn_ready"), sem("cT_ps"), sem("cT_ready")
        o_ps, x1_ready = sem("o_ps"), sem("x1_ready")
        xn_ready = sem("xn_ready")
        xT_ps, xT_hi_ready, xT_lo_ready = sem("xT_ps"), sem("xT_hi_ready"), sem("xT_lo_ready")
        xrT_ps, xrT_ready = sem("xrT_ps"), sem("xrT_ready")
        logit_ps, logit_read, lexp_ready, comb_ready = sem("logit_ps"), sem("logit_read"), sem("lexp_ready"), sem("comb_ready")
        combT_ps, combT_ready, spread_done, spread_ready = (sem(n) for n in ("combT_ps", "combT_ready", "spread_done", "spread_ready"))
        gate_done, silu_done, scaled, up_done = sem("gate_done"), sem("silu_done"), sem("scaled"), sem("up_done")
        hid_done, hi_done, lo_done, down_done = sem("hid_done"), sem("hi_done"), sem("lo_done"), sem("down_done")
        pool_lo = sem("pool_lo")
        last_hid, last_hi, last_lo = sem("last_hid"), sem("last_hi"), sem("last_lo")
        y_ready = sem("y_ready")

        aw = {n: attw_sb[:, a:b] for n, (a, b) in AW.items()}
        cc = {n: c1_sb[:, a:b] for n, (a, b) in C1.items()} | {n: c2_sb[:, a:b] for n, (a, b) in C2.items()}
        ident = cc["ident"]
        identb, mask01, mask2 = cb[:, 0:P], cb[:, P:P + S_CTX], cb[:, P + S_CTX:CB_W]
        nk = NB * S_CTX

        def gate_bank(m):
            return att[0] if m > NCH and (m - NCH) % 2 else gate_ps

        def width(c):
            return NARROW if c == NSH - 1 else P

        def wait_low(engine, m):
            if m in POOL_LOW:
                engine.wait_ge(pool_lo, POOL_LOW.index(m) + 1)
            else:
                engine.wait_ge(lo_done, m + 1 - sum(n < m for n in POOL_LOW))

        def scaled_before(m):
            g, c = divmod(m, NCH)
            return g * NEXP + max(c - NSH, 0)

        def batches(t):
            return [(t, 0, P)] if t < 2 else [(0, 0, 32), (1, 32, 64)]

        block = ctx.enter_context(nc.Block())

        @block.sync
        def _(sp):
            sp.dma_start(xr[:, 3:7, :], x[:, 3:7, :]).then_inc(ld_xf, 16)
            sp.dma_start(c1_sb[:], c1).then_inc(ld_c1, 16)
            sp.dma_start(w[:, 0:1, :], wall[:, 0:1, :]).then_inc(ld_w[0], 16)
            sp.dma_start(c2_sb[:], c2).then_inc(ld_c2, 16)
            for i, (a, b) in list(enumerate(W_LOADS))[1:]:
                sp.dma_start(w[:, a:b, :], wall[:, a:b, :]).then_inc(ld_w[i], 16)
                if i == 1:
                    sp.dma_start(vb[:], rows[1:2, :].partition_broadcast(P)).then_inc(ld_vb, 16)
                if i == 2:
                    sp.dma_start(sel_sb[:], sel).then_inc(ld_sel, 16)
                    sp.dma_start(cb[:], cbf).then_inc(ld_cb, 16)
                if i == 3:
                    sp.dma_start(xr[:, 7:8, :], x[:, 7:8, :]).then_inc(ld_x7, 16)
            for g in range(2):
                for half in range(2):
                    sp.wait_ge(y_ready, 2 * g + half + 1)
                    cols = slice(256 * half, 256 * half + 256)
                    sp.dma_start(out[:, g, cols], xrT[:, g, cols]).then_inc(stored, 16)
            sp.wait_ge(stored, 16 * 4)

        @block.gpsimd
        def _(pool):
            n_raw, n_var = [0], [0]

            def then(ins):
                n_raw[0] += 1
                ins.then_inc(pool_raw, 1)
                pool.wait_ge(pool_raw, n_raw[0])

            def make_rstd(a, b):
                n_var[0] += 1
                pool.wait_ge(var_ready, n_var[0])
                then(nc.gpsimd.tensor_scalar(rstd[:, a:b], mv[:, a:b, 1], LN_EPS, None, ALU.add))
                nc.gpsimd.tensor_tensor(rstd[:, a:b], rstd[:, a:b], cc["half"][:, 0:b - a], ALU.pow).then_inc(rstd_ready, 1)

            def weights_low(c):
                pool.wait_ge(w_hi_ready, c + 1)
                nc.gpsimd.tensor_tensor(w_lo[:, c, :], w[:, c, :], w_hi[:, c, :].bitcast(F32), ALU.subtract).then_inc(w_lo_ready, 1)

            def block_keys(b):
                pool.wait_ge(kT_ready, 1)
                nc.gpsimd.tensor_tensor(kbd[:, b], kT[:, None, b * S_CTX:(b + 1) * S_CTX].to_broadcast([P, H, S_CTX]),
                                        cc["m16"][:, :, None].to_broadcast([P, H, S_CTX]), ALU.mult).then_inc(kbd_ready, 1)

            def block_last_values():
                pool.wait_ge(v_ready, 1)
                m8 = cc["m8"][0:R2, None, :]
                bd = vbd2[:].rearrange("r b j h d -> r (b j) h d")
                nc.gpsimd.tensor_copy(bd[:, :, :, DH], m8.to_broadcast([R2, 2 * NB, H2]))
                nc.gpsimd.tensor_tensor(bd[:, :, :, 0:DH], v2[:].rearrange("r b (j h d) -> r (b j) h d", j=2, h=H2),
                                        m8[:, :, :, None].to_broadcast([R2, 2 * NB, H2, DH]), ALU.mult).then_inc(v2_ready, 1)

            def hidden_low(m):
                pool.wait_ge(hi_done, m + 1)
                pool.wait_ge(down_done, m - 3)
                nc.gpsimd.tensor_tensor(hid_lo[:, m % 4, :], hid[:, m % 3, :], hid_hi[:, m % 4, :].bitcast(F32),
                                        ALU.subtract).then_inc(pool_lo, 1)

            pool.wait_ge(ld_xf, 16)
            pool.wait_ge(ld_ob, 16)
            nc.gpsimd.tensor_tensor(xr[:, 5:7, :], xr[:, 5:7, :], ob[:, None, :].to_broadcast([P, 2, D]), ALU.add).then_inc(pool_added, 1)
            pool.wait_ge(ld_c1, 16)
            make_rstd(3, 7)
            make_rstd(NT, NT + 3)
            pool.wait_ge(ld_attw, 16)
            then(nc.gpsimd.tensor_copy(gw_hl[:, 0:E], aw["gw"]))
            nc.gpsimd.tensor_tensor(gw_hl[:, E:2 * E], aw["gw"], gw_hl[:, 0:E].bitcast(F32), ALU.subtract).then_inc(pool_gw, 1)
            weights_low(1)
            weights_low(2)
            block_keys(0)
            for m in range(2 * NCH):
                c = m % NCH
                if c >= NSH:
                    pool.wait_ge(silu_done, m + 1)
                    pool.wait_ge(spread_ready, scaled_before(m) + 1)
                    if m >= 3:
                        pool.wait_ge(hid_done, m - 2)
                    nc.gpsimd.tensor_tensor(sc[:, m % 3, :], sg[:, m % 3, :], spread[:, c - NSH, :],
                                            ALU.mult).then_inc(scaled, 1)
                for c in SPLIT_AT.get(m, []):
                    weights_low(c)
                if m - 1 in POOL_LOW:
                    hidden_low(m - 1)
                if m == 0:
                    block_keys(1)
                if m == 3:
                    block_last_values()
                if m == 7:
                    make_rstd(7, 8)
                for t in range(3):
                    if m == steps_at("project", t) // 2:
                        make_rstd(t, t + 1)

        @block.scalar
        def _(act):
            act.dma_start(ob[:], rows[0:1, :].partition_broadcast(P)).then_inc(ld_ob, 16)
            act.dma_start(xr[:, 0:3, :], x[:, 0:3, :]).then_inc(ld_xa, 16)
            act.dma_start(attw_sb[:], attw).then_inc(ld_attw, 16)

            def weights_high(c):
                if c in [a for a, _ in W_LOADS]:
                    act.wait_ge(ld_w[[a for a, _ in W_LOADS].index(c)], 16)
                nc.scalar.copy(w_hi[:, c, :], w[:, c, :]).then_inc(w_hi_ready, 1)

            def xT_high(g):
                act.wait_ge(xT_ps, g + 1)
                nc.scalar.copy(xT_hi[:, g, :], att[0][:, :]).then_inc(xT_hi_ready, 1)

            def xrT_copy(g):
                act.wait_ge(xrT_ps, g + 1)
                nc.scalar.copy(xrT[:, g, :], att[2][:, :]).then_inc(xrT_ready, 1)

            def route_exp(g):
                act.wait_ge(logit_read, g + 1)
                nc.scalar.activation(lexp[:, g], lexp[:, g], ACT.Exp).then_inc(lexp_ready, 1)

            def combT_copy(g):
                act.wait_ge(combT_ps, g + 1)
                nc.scalar.copy(combT[:, g, :], spread_ps[0][0:2 * E, :]).then_inc(combT_ready, 1)

            def spread_copy(n):
                act.wait_ge(spread_done, n + 1)
                if n >= NEXP:
                    act.wait_ge(scaled, n - NEXP + 1)
                nc.scalar.copy(spread[:, n % NEXP, :], spread_ps[n % NEXP % 2][:, :]).then_inc(spread_ready, 1)

            def attend_exp(steps):
                for s in steps:
                    p = prob[:, s] if s < 8 else prob2[:]
                    act.wait_ge(scores_read, s + 1)
                    nc.scalar.activation(p, p, ACT.Exp).then_inc(prob_ready, 1)

            def select(n):
                part = slice(SEL_PARTS[n], SEL_PARTS[n + 1])
                act.wait_ge(ld_sel, 16)
                nc.scalar.copy(sel_r[:, part, :], sel_sb[:, part, :]).then_inc(sel_ready, 1)

            def silu(m):
                wc = width(m % NCH)
                act.wait_ge(gate_done, m + 1)
                if m >= 3:
                    act.wait_ge(hid_done, m - 2)
                nc.scalar.activation(sg[0:wc, m % 3, :], gate_bank(m)[0:wc, :], ACT.Silu).then_inc(silu_done, 1)

            def hidden_high(m):
                wc = width(m % NCH)
                act.wait_ge(hid_done, m + 1)
                if m >= 4:
                    act.wait_ge(down_done, m - 3)
                nc.scalar.copy(hid_hi[0:wc, m % 4, :], hid[0:wc, m % 3, :]).then_inc(hi_done, 1)

            def ctxT_copy(t):
                r = ATT_ROWS[t]
                act.wait_ge(cT_ps, t + 1)
                nc.scalar.copy(cT[:, t, 0:r], ctx_ps[t][:, TC:TC + r]).then_inc(cT_ready, 1)

            weights_high(0)
            xT_high(0)
            weights_high(1)
            weights_high(2)
            act.wait_ge(xn1T_ps, 1)
            nc.scalar.copy(xn1T[:], down_ps[:, 0:NQ]).then_inc(xn1T_ready, 1)
            route_exp(0)
            for m in range(2 * NCH):
                if m == EXP_UNIT:
                    attend_exp(range(3, 9))
                if m == NCH:
                    route_exp(1)
                    hidden_high(m - 1)
                silu(m)
                for i in (2 * m, 2 * m + 1):
                    if i == 2 * EXP_UNIT - 1:
                        attend_exp(range(3))
                    spread_at(i, spread_copy)
                    for step, n in ATTENTION.get(i, []):
                        if step == "turn_ctx":
                            ctxT_copy(n)
                if m == NCH - 1:
                    xT_high(1)
                if m in SEL_UNITS:
                    select(SEL_UNITS.index(m))
                for c in SPLIT_AT.get(m, []):
                    weights_high(c)
                if 2 * m + 2 in COMB_AT:
                    combT_copy(m // NCH)
                if m not in (0, NCH):
                    hidden_high(m - 1)
                if m % NCH == 0:
                    xrT_copy(m // NCH)
            for h, cols in enumerate(HALVES):
                act.wait_ge(last_hid, h + 1)
                nc.scalar.copy(last_hid_hi[:, cols], hid[:, LAST % 3, cols]).then_inc(last_hi, 1)

        @block.vector
        def _(dve):
            n_raw, n_rstd = [0], [0]

            def mark(ins):
                n_raw[0] += 1
                ins.then_inc(dve_raw, 1)
                return n_raw[0]

            def then(ins):
                dve.wait_ge(dve_raw, mark(ins))

            def norm_stats(tiles, at):
                for i, t in enumerate(tiles):
                    last = nc.vector.bn_stats(stats[:, at + i, :], xr[:, t, :])
                then(last)
                for i in range(len(tiles)):
                    last = nc.vector.bn_aggr(mv[:, at + i, :], stats[:, at + i, :])
                last.then_inc(var_ready, 1)

            def normalise(tiles, at):
                n_rstd[0] += 1
                dve.wait_ge(rstd_ready, n_rstd[0])
                for i, t in enumerate(tiles):
                    last = nc.vector.tensor_scalar(xn[:, at + i, :], xr[:, t, :], mv[:, at + i, 0:1],
                                                   rstd[:, at + i:at + i + 1], ALU.subtract, ALU.mult)
                    if at < NT:
                        last.then_inc(xn_ready, 1)
                return last

            def add_ob(a, b):
                return nc.vector.tensor_tensor(xr[:, a:b, :], xr[:, a:b, :],
                                               ob[:, None, :].to_broadcast([P, b - a, D]), ALU.add)

            def xT_low(g):
                dve.wait_ge(xT_hi_ready, g + 1)
                nc.vector.tensor_tensor(xT_lo[:, g, :], att[0][:, :], xT_hi[:, g, :].bitcast(F32),
                                        ALU.subtract).then_inc(xT_lo_ready, 1)

            def logit_bank(g):
                return (up_ps[1], att[1])[g][:, 0:8 * E]

            def route_sub(g):
                dve.wait_ge(logit_ps, g + 1)
                then(nc.vector.tensor_reduce(lg[:, g], logit_bank(g).rearrange("p (t s e) -> p t e s", t=4, s=2), AX.X, ALU.add))
                then(nc.vector.tensor_reduce(lmax[:, g, :], lg[:, g], AX.X, ALU.max))
                nc.vector.tensor_tensor(lexp[:, g], lg[:, g], lmax[:, g, :, None].to_broadcast([P, 4, E]),
                                        ALU.subtract).then_inc(logit_read, 1)

            def route(g):
                dve.wait_ge(lexp_ready, g + 1)
                flat = ldif[:, g].rearrange("p t e j -> p t (e j)")
                summed = mark(nc.vector.tensor_reduce(lsum[:, g, :], lexp[:, g], AX.X, ALU.add))
                differ = mark(nc.vector.tensor_tensor(ldif[:, g], lexp[:, g, :, None, :].to_broadcast([P, 4, E, E]),
                                                      lexp[:, g, :, :, None].to_broadcast([P, 4, E, E]), ALU.subtract))
                dve.wait_ge(dve_raw, summed)
                inverse = mark(nc.vector.reciprocal(lrec[:, g, :], lsum[:, g, :]))
                dve.wait_ge(dve_raw, differ)
                before = mark(nc.vector.tensor_tensor(flat, flat, cc["thr"][:, None, :].to_broadcast([P, 4, E * E]), ALU.is_ge))
                dve.wait_ge(dve_raw, inverse)
                nc.vector.tensor_tensor(lp[:, g], lexp[:, g], lrec[:, g, :, None].to_broadcast([P, 4, E]), ALU.mult)
                dve.wait_ge(dve_raw, before)
                then(nc.vector.tensor_reduce(lrank[:, g], ldif[:, g], AX.X, ALU.add))
                then(nc.vector.scalar_tensor_tensor(out=lsel[:, g], in0=lrank[:, g], scalar=1.5, in1=lp[:, g],
                                                    op0=ALU.is_lt, op1=ALU.mult))
                then(nc.vector.tensor_reduce(tsum[:, g, :], lsel[:, g], AX.X, ALU.add))
                then(nc.vector.tensor_scalar(tsum[:, g, :], tsum[:, g, :], TOP_EPS, None, ALU.add))
                then(nc.vector.reciprocal(trec[:, g, :], tsum[:, g, :]))
                then(nc.vector.scalar_tensor_tensor(out=comb[:, g], in0=lsel[:, g], scalar=TOP_SCALE,
                                                    in1=trec[:, g, :, None].to_broadcast([P, 4, E]),
                                                    op0=ALU.mult, op1=ALU.mult))
                then(nc.vector.tensor_copy(comb2[:, g, :, 0:E].bitcast(F32R), comb[:, g]))
                nc.vector.tensor_tensor(comb2[:, g, :, E:2 * E], comb[:, g], comb2[:, g, :, 0:E],
                                        ALU.subtract).then_inc(comb_ready, 1)

            def rope(dst, b, in1, in2, bias1, bias2, cos, sin):
                nc.vector.scalar_tensor_tensor(out=dst, in0=in1, scalar=bias1, in1=cos, op0=ALU.add, op1=ALU.mult)
                then(nc.vector.scalar_tensor_tensor(out=b, in0=in2, scalar=bias2, in1=sin, op0=ALU.add, op1=ALU.mult))
                return nc.vector.tensor_tensor(dst, dst, b, ALU.add)

            def keys():
                dve.wait_ge(k_ps, 1)
                dve.wait_ge(ld_c2, 16)
                rope(kT[:], k2[:], att[1][:, 0:nk], att[1][:, nk:2 * nk],
                     aw["bias"][:, 2:3], aw["bias"][:, 3:4], cc["cosk"], cc["sink"]).then_inc(kT_ready, 1)

            def queries():
                dve.wait_ge(q_ps, 1)
                rope(qT[:], q2[:], down_ps[:, 0:NQ], att[0][:, 0:NQ],
                     aw["bias"][:, 0:1], aw["bias"][:, 1:2], cc["cosq"], cc["sinq"]).then_inc(q_ready, 1)

            def values():
                dve.wait_ge(v_ps, 1)
                dve.wait_ge(ld_vb, 16)
                nc.vector.tensor_tensor(v2[:], spread_ps[0][0:R2, NB * D:2 * NB * D].rearrange("k (b d) -> k b d", b=NB),
                                        vb[0:R2, None, :].to_broadcast([R2, NB, D]), ALU.add)
                for b in range(NB):
                    last = nc.vector.tensor_tensor(
                        vaug[:, b, :, 0:DH],
                        spread_ps[0][0:S_CTX, b * D:(b + 1) * D].rearrange("k (h d) -> k h d", h=H),
                        vb[0:S_CTX, :].rearrange("k (h d) -> k h d", h=H), ALU.add)
                last.then_inc(v_ready, 1)

            def softmax_max(s):
                dve.wait_ge(scores_done, s + 1)
                if s < 8:
                    sc_ = scores_ps[s % 2][:, 0:4 * S_CTX].rearrange("q (h k) -> q h k", h=4)
                    top, dst, shape = smax[:, s, :], prob[:, s], [P, 4, S_CTX]
                else:
                    sc_ = scores_ps[s % 2][0:64, 0:H * NK2].rearrange("q (h k) -> q h k", h=H)
                    top, dst, shape = smax2[:], prob2[:], [64, H, NK2]
                then(nc.vector.tensor_reduce(top, sc_, AX.X, ALU.max))
                nc.vector.tensor_tensor(dst, sc_, top[:, :, None].to_broadcast(shape), ALU.subtract).then_inc(scores_read, 1)

            def probT_copy(p):
                dve.wait_ge(pT_done, p + 1)
                if p >= 2:
                    dve.wait_ge(ctx_done, p - 1)
                r, n = (S_CTX, 4 * P) if p < 8 else (R2, 2 * 64)
                nc.vector.tensor_copy(probT[0:r, p % 2, 0:n], pT_ps[p % 2][0:r, 0:n]).then_inc(pT_read, 1)

            def ctx_norm(t):
                r = ATT_ROWS[t]
                dve.wait_ge(ctx_done, (4, 8, 9)[t])
                cv = ctx_ps[t][0:r, 0:H * (DH + 1)].rearrange("q (h d) -> q h d", h=H)
                then(nc.vector.reciprocal(rden[0:r, t, :], cv[:, :, DH]))
                nc.vector.tensor_tensor(cn[0:r, t, :].rearrange("q (h d) -> q h d", h=H), cv[:, :, 0:DH],
                                        rden[0:r, t, :, None].to_broadcast([r, H, DH]), ALU.mult).then_inc(cn_ready, 1)

            def add_attention(t):
                r = ATT_ROWS[t]
                dve.wait_ge(o_ps, t + 1)
                scalar = 1.0 if t < 2 else cc["valid"][0:r, :]
                ins = nc.vector.scalar_tensor_tensor(out=xr[0:r, t, :], in0=ctx_ps[t][0:r, PC:PC + D], scalar=scalar,
                                                     in1=xr[0:r, t, :], op0=ALU.mult, op1=ALU.add)
                ins.then_inc(x1_ready, 1)
                dve.wait_ge(x1_ready, t + 1)
                norm_stats([t], t)

            def hidden(m):
                g, c = divmod(m, NCH)
                wc = width(c)
                if c >= NSH:
                    dve.wait_ge(scaled, scaled_before(m) + 1)
                else:
                    dve.wait_ge(silu_done, m + 1)
                dve.wait_ge(up_done, m + 1)
                if m >= 3:
                    dve.wait_ge(hi_done, m - 2)
                    wait_low(dve, m - 3)
                s = (sc if c >= NSH else sg)[0:wc, m % 3, :]
                nc.vector.tensor_tensor(hid[0:wc, m % 3, :], s, up_ps[m % 2][0:wc, :], ALU.mult).then_inc(hid_done, 1)

            def hidden_low(m):
                wc = width(m % NCH)
                dve.wait_ge(hi_done, m + 1)
                if m >= 4:
                    dve.wait_ge(down_done, m - 3)
                nc.vector.tensor_tensor(hid_lo[0:wc, m % 4, :], hid[0:wc, m % 3, :],
                                        hid_hi[0:wc, m % 4, :].bitcast(F32), ALU.subtract).then_inc(lo_done, 1)

            def hidden_last():
                m, s = LAST, LAST % 3
                dve.wait_ge(scaled, 2 * NEXP)
                dve.wait_ge(up_done, m + 1)
                dve.wait_ge(hi_done, m - 2)
                wait_low(dve, m - 3)
                for cols in HALVES:
                    nc.vector.tensor_tensor(hid[:, s, cols], sc[:, s, cols], up_ps[m % 2][:, cols], ALU.mult).then_inc(last_hid, 1)
                for h, cols in enumerate(HALVES):
                    dve.wait_ge(last_hi, h + 1)
                    nc.vector.tensor_tensor(last_hid_lo[:, cols], hid[:, s, cols], last_hid_hi[:, cols].bitcast(F32),
                                            ALU.subtract).then_inc(last_lo, 1)

            def finish(g):
                dve.wait_ge(down_done, NCH * (g + 1))
                dve.wait_ge(xrT_ready, g + 1)
                for half in range(2):
                    cols = slice(256 * half, 256 * half + 256)
                    nc.vector.tensor_tensor(xrT[:, g, cols], down_ps[:, cols], xrT[:, g, cols], ALU.add).then_inc(y_ready, 1)

            nc.vector.memset(vaug[:], 1.0)
            dve.wait_ge(ld_xf, 16)
            dve.wait_ge(ld_ob, 16)
            added = mark(add_ob(3, 5))
            dve.wait_ge(dve_raw, added)
            for t in range(3, 7):
                if t == 5:
                    dve.wait_ge(pool_added, 1)
                last = nc.vector.bn_stats(stats[:, t, :], xr[:, t, :])
            then(last)
            for t in range(3, 7):
                last = nc.vector.bn_aggr(mv[:, t, :], stats[:, t, :])
            last.then_inc(var_ready, 1)
            dve.wait_ge(ld_xa, 16)
            norm_stats([0, 1, 2], NT)
            normalise([3, 4, 5, 6], 3)
            dve.wait_ge(w_hi_ready, 1)
            nc.vector.tensor_tensor(w_lo[:, 0, :], w[:, 0, :], w_hi[:, 0, :].bitcast(F32),
                                    ALU.subtract).then_inc(w0_lo_ready, 1)
            normalise([0, 1, 2], NT).then_inc(xn1_ready, 1)
            xT_low(0)
            keys()
            route_sub(0)
            dve.wait_ge(xn1_ready, 1)
            add_ob(0, 3)
            values()
            route(0)

            for m in range(2 * NCH):
                g, c = divmod(m, NCH)
                if m == NCH:
                    route(1)
                if m == NCH + 2:
                    finish(0)
                for i in (2 * m, 2 * m + 1):
                    for step, n in ATTENTION.get(i - 2, []):
                        if step == "project":
                            normalise([n], n)
                    for step, n in ATTENTION.get(i, []):
                        if step == "scores":
                            softmax_max(n)
                        if step == "turn_probs":
                            probT_copy(n)
                        if step == "context" and n in (3, 7, 8):
                            ctx_norm(min(n // 4, 2))
                        if step == "project":
                            add_attention(n)
                if m == 9:
                    normalise([7], 7)
                if m == LAST:
                    hidden_last()
                    break
                if m == LAST - 1:
                    hidden_low(m - 1)
                hidden(m)
                if m == NCH - 2:
                    xT_low(1)
                if m == NCH - 1:
                    route_sub(1)
                if m not in (0, NCH, LAST - 1):
                    hidden_low(m - 1)
                if m == 0:
                    queries()
                if m == 7:
                    dve.wait_ge(ld_x7, 16)
                    then(add_ob(7, 8))
                    norm_stats([7], 7)
            finish(1)

        @block.tensor
        def _(pe):
            def turn_x(g):
                for i, t in enumerate(GROUPS[g]):
                    pe.wait_ge(xn_ready, 4 * g + i + 1)
                    last = nc.tensor.transpose(att[0][:, i * P:(i + 1) * P], xn[:, t, :], ident)
                last.then_inc(xT_ps, 1)

            def turn_xr(g):
                for i, t in enumerate(GROUPS[g]):
                    last = nc.tensor.transpose(att[2][:, i * P:(i + 1) * P], xr[:, t, :], ident)
                last.then_inc(xrT_ps, 1)

            def logits(g):
                bl = (up_ps[1], att[1])[g]
                pe.wait_ge(xT_lo_ready, g + 1)
                for i in range(4):
                    o, c = bl[:, 2 * i * E:2 * (i + 1) * E], slice(i * P, (i + 1) * P)
                    nc.tensor.matmul(o, xT_hi[:, g, c], gw_hl[:], start=True, stop=False)
                    last = nc.tensor.matmul(o, xT_lo[:, g, c], gw_hl[:], start=False, stop=True)
                last.then_inc(logit_ps, 1)

            def turn_comb(g):
                pe.wait_ge(comb_ready, g + 1)
                if g == 0:
                    pe.wait_ge(v_ready, 1)
                for i in range(4):
                    last = nc.tensor.transpose(spread_ps[0][0:2 * E, i * P:(i + 1) * P], comb2[:, g, i, :], ident)
                last.then_inc(combT_ps, 1)

            def spread_comb(n):
                g, c = divmod(n, NEXP)
                if c == 0:
                    pe.wait_ge(combT_ready, g + 1)
                    pe.wait_ge(xrT_ready, g + 1)
                if c >= 2:
                    pe.wait_ge(spread_ready, n - 1)
                if g == 0 and c in SEL_PARTS:
                    pe.wait_ge(sel_ready, SEL_PARTS.index(c) + 1)
                nc.tensor.matmul(spread_ps[c % 2][:, :], sel_r[:, c, :], combT[:, g, :], start=True, stop=True).then_inc(spread_done, 1)

            def product(dst, c, cols, g, done):
                wh, wl = w_hi[:, c, cols], w_lo[:, c, cols]
                nc.tensor.matmul(dst, wh, xT_hi[:, g, :], start=True, stop=False)
                nc.tensor.matmul(dst, wh, xT_lo[:, g, :], start=False, stop=False)
                nc.tensor.matmul(dst, wl, xT_hi[:, g, :], start=False, stop=True).then_inc(done, 1)

            def gate(m):
                g, c = divmod(m, NCH)
                wc = width(c)
                if m == 0:
                    pe.wait_ge(w0_lo_ready, 1)
                elif g == 0:
                    pe.wait_ge(w_lo_ready, c)
                if c == 0:
                    pe.wait_ge(xT_lo_ready, g + 1)
                if 1 <= m <= NCH:
                    pe.wait_ge(silu_done, m)
                elif m > NCH + 1:
                    pe.wait_ge(silu_done, m - 1)
                product(gate_bank(m)[0:wc, :], c, slice(0, wc), g, gate_done)

            def up(m):
                g, c = divmod(m, NCH)
                wc = width(c)
                if m == 1:
                    pe.wait_ge(logit_read, 1)
                if m >= 2:
                    pe.wait_ge(hid_done, m - 1)
                product(up_ps[m % 2][0:wc, :], c, slice(P, P + wc), g, up_done)

            def down(m):
                down_high(m)
                down_low(m)

            def down_high(m):
                c = m % NCH
                wc = width(c)
                wh, wl = w_hi[0:wc, c, 2 * P:3 * P], w_lo[0:wc, c, 2 * P:3 * P]
                if m == 0:
                    pe.wait_ge(q_ready, 1)
                if m == NCH:
                    pe.wait_ge(y_ready, 2)
                pe.wait_ge(hi_done, m + 1)
                for wx in (wh, wl):
                    nc.tensor.matmul(down_ps[:, :], wx, hid_hi[0:wc, m % 4, :], start=(c == 0 and wx is wh), stop=False)

            def down_low(m):
                c = m % NCH
                wc = width(c)
                wait_low(pe, m)
                nc.tensor.matmul(down_ps[:, :], w_hi[0:wc, c, 2 * P:3 * P], hid_lo[0:wc, m % 4, :],
                                 start=False, stop=(c == NCH - 1)).then_inc(down_done, 1)

            def down_end():
                down_high(LAST - 1)
                wh, wl = w_hi[:, NCH - 1, 2 * P:3 * P], w_lo[:, NCH - 1, 2 * P:3 * P]
                for h, cols in enumerate(HALVES):
                    pe.wait_ge(last_hi, h + 1)
                    for wx in (wh, wl):
                        nc.tensor.matmul(down_ps[:, cols], wx, last_hid_hi[:, cols], start=False, stop=False, skip_group_check=True)
                down_low(LAST - 1)
                pe.wait_ge(last_lo, 2)
                nc.tensor.matmul(down_ps[:, :], wh, last_hid_lo, start=False, stop=True).then_inc(down_done, 1)

            def scores(s):
                t, g = STEPS[s]
                dst = scores_ps[s % 2]
                if s == 0:
                    pe.wait_ge(ld_cb, 16)
                    pe.wait_ge(kbd_ready, 1)
                    pe.wait_ge(q_ready, 1)
                if s == 4:
                    pe.wait_ge(kbd_ready, 2)
                if s >= 2:
                    pe.wait_ge(scores_read, s - 1)
                if t < 2:
                    nc.tensor.matmul(dst[:, 0:4 * S_CTX], identb, mask01[:, None, :].to_broadcast([P, 4, S_CTX]),
                                     start=True, stop=False, skip_group_check=True)
                    nc.tensor.matmul(dst[:, 0:4 * S_CTX], qT[:, QCOL[t]:QCOL[t] + P],
                                     kbd[:, t, 4 * g:4 * g + 4, :].rearrange("p h k -> p (h k)"),
                                     start=False, stop=True, skip_group_check=True).then_inc(scores_done, 1)
                    return
                nc.tensor.matmul(dst[0:64, 0:H * NK2], identb[0:64, 0:64], mask2[0:64, None, :].to_broadcast([64, H, NK2]),
                                 start=True, stop=False, skip_group_check=True)
                for b, q0, q1_ in batches(t):
                    last = nc.tensor.matmul(dst[q0:q1_, 0:H * NK2], qT[:, QCOL[t] + q0:QCOL[t] + q1_],
                                            kbd[:, b, :, KEY2:S_CTX], start=False, stop=True, skip_group_check=True)
                last.then_inc(scores_done, 1)

            def turn_probs(p):
                pe.wait_ge(prob_ready, p + 1 if p < 8 else 9)
                if p == 0:
                    pe.wait_ge(scores_read, 9)
                    pe.wait_ge(spread_ready, NEXP)
                if p >= 2:
                    pe.wait_ge(pT_read, p - 1)
                if p < 8:
                    for hh in range(4):
                        last = nc.tensor.transpose(pT_ps[p % 2][0:S_CTX, hh * P:(hh + 1) * P], prob[:, p, hh, :], ident)
                else:
                    for j in range(2):
                        last = nc.tensor.transpose(pT_ps[p % 2][0:R2, j * 64:(j + 1) * 64],
                                                   prob2[:, j * H2:(j + 1) * H2, :].rearrange("q h k -> q (h k)"), ident[0:64, 0:64])
                last.then_inc(pT_done, 1)

            def context(p):
                t = min(p // 4, 2)
                pe.wait_ge(pT_read, p + 1)
                if p == 8:
                    pe.wait_ge(x1_ready, 1)
                    pe.wait_ge(v2_ready, 1)
                    for b, q0, q1_ in batches(t):
                        for j in range(2):
                            w_ = H2 * (DH + 1)
                            last = nc.tensor.matmul(ctx_ps[t][q0:q1_, j * w_:(j + 1) * w_],
                                                    probT[0:R2, p % 2, j * 64 + q0:j * 64 + q1_],
                                                    vbd2[:, b, j].rearrange("r h d -> r (h d)"), start=True, stop=True)
                else:
                    for hh in range(4):
                        h = 4 * (p % 4) + hh
                        last = nc.tensor.matmul(ctx_ps[t][:, h * (DH + 1):(h + 1) * (DH + 1)],
                                                probT[0:S_CTX, p % 2, hh * P:(hh + 1) * P], vaug[:, t, h, :],
                                                start=True, stop=True)
                last.then_inc(ctx_done, 1)

            def turn_ctx(t):
                r = ATT_ROWS[t]
                pe.wait_ge(cn_ready, t + 1)
                nc.tensor.transpose(ctx_ps[t][:, TC:TC + r], cn[0:r, t, :], ident[0:r, 0:r]).then_inc(cT_ps, 1)

            def project_out(t):
                r = ATT_ROWS[t]
                pe.wait_ge(cT_ready, t + 1)
                nc.tensor.matmul(ctx_ps[t][0:r, PC:PC + D], cT[:, t, 0:r], aw["ow"], start=True, stop=True).then_inc(o_ps, 1)

            pe.wait_ge(ld_attw, 16)
            nc.tensor.matmul(att[1][:, 0:nk], aw["kw"], aw["ctxT"], start=True, stop=True)
            nc.tensor.matmul(att[1][:, nk:2 * nk], aw["kws"], aw["ctxT"], start=True, stop=True).then_inc(k_ps, 1)
            pe.wait_ge(ld_c1, 16)
            turn_x(0)
            for keys_T, r, at in (("ctxT", S_CTX, 0), ("ctx2T", R2, NB * D)):
                for b in range(NB):
                    last = nc.tensor.matmul(spread_ps[0][0:r, at + b * D:at + (b + 1) * D],
                                            aw[keys_T][:, b * r:(b + 1) * r], aw["vw"], start=True, stop=True)
            last.then_inc(v_ps, 1)
            pe.wait_ge(pool_gw, 1)
            logits(0)
            pe.wait_ge(xn1_ready, 1)
            for t in range(3):
                r = ATT_ROWS[t]
                last = nc.tensor.transpose(down_ps[:, QCOL[t]:QCOL[t] + r], xn[0:r, NT + t, :], ident[0:r, 0:r])
            last.then_inc(xn1T_ps, 1)
            turn_xr(0)
            for m in range(2 * NCH):
                g, c = divmod(m, NCH)
                for i in (2 * m, 2 * m + 1):
                    if i in COMB_AT:
                        turn_comb(g)
                    if i % 2 == 0:
                        gate(m)
                    else:
                        up(m)
                    if i == 1:
                        pe.wait_ge(xn1T_ready, 1)
                        nc.tensor.matmul(down_ps[:, 0:NQ], aw["qw"], xn1T[:], start=True, stop=True)
                        nc.tensor.matmul(att[0][:, 0:NQ], aw["qws"], xn1T[:], start=True, stop=True).then_inc(q_ps, 1)
                    if i == 2 * NCH - 2:
                        turn_x(1)
                    spread_at(i, spread_comb)
                    for step, n in ATTENTION.get(i, []):
                        {"scores": scores, "turn_probs": turn_probs, "context": context,
                         "turn_ctx": turn_ctx, "project": project_out, "down": down}[step](n)
                for n in {EXP_UNIT: [], NCH: [m - 3, m - 2], NCH + 1: [m - 2], NCH + 2: [],
                          2 * NCH - 2: [], 2 * NCH - 1: [m - 4, m - 3, m - 2]}.get(m, [m - 3]):
                    if n >= 0:
                        down(n)
                if m == NCH - 1:
                    turn_xr(1)
                    logits(1)
            down_end()


SPLIT_AT = {0: [3, 4], 3: [5], 4: [6], 5: [7, 8], 7: [9], 8: [10], 9: [11], 10: [12, 13]}
COMB_AT = [4, 2 * NCH + 4]
SEL_PARTS = [0, 3, 7, NEXP]
SEL_UNITS = [0, 1, 3]
SPREAD_AT = [[5, 6, 6, 7, 7, 8, 9, 9, 10, 11, 12],
             [5, 6, 7, 8, 9, 10, 11, 12, 13, 14, 15]]
EXP_UNIT = 7
SCORES_AT = [7, 8, 8, 9, 10, 10, 11, 12, 12]
ATTENTION = {i: [("scores", n) for n in range(9) if SCORES_AT[n] == i] for i in SCORES_AT} | {
    15: [("turn_probs", 0), ("turn_probs", 1), ("down", EXP_UNIT - 3), ("context", 0),
         ("turn_probs", 2), ("context", 1), ("turn_probs", 3), ("context", 2)],
    16: [("turn_probs", 4), ("context", 3)],
    17: [("turn_probs", 5), ("context", 4)],
    18: [("turn_probs", 6), ("context", 5), ("turn_ctx", 0)],
    19: [("turn_probs", 7), ("context", 6), ("project", 0)],
    20: [("turn_probs", 8), ("context", 7)],
    21: [("context", 8), ("turn_ctx", 1)],
    22: [("project", 1), ("turn_ctx", 2)],
    23: [("project", 2)],
}


def steps_at(step, n):
    return [i for i, steps in ATTENTION.items() if (step, n) in steps][0]


def spread_at(i, spread_one):
    g, j = divmod(i, 2 * NCH)
    for e, at in enumerate(SPREAD_AT[g]):
        if at == j:
            spread_one(g * NEXP + e)


def positions(tile):
    return np.concatenate([np.arange(p, p + n) for _, p, n in TILES[tile]])


def rope_tables(pos, scale):
    half = DH // 2
    freqs = np.float32(1.0) / np.float32(10000.0) ** (np.arange(half, dtype=np.float32) / np.float32(half))
    ang = pos.astype(np.float32)[None, :] * freqs[:, None]
    cos, sin = np.cos(ang), np.sin(ang)
    cos = np.tile(np.concatenate([cos, cos]), (H, 1)) * scale
    sin = np.tile(np.concatenate([-sin, sin]), (H, 1)) * scale
    return cos.astype(np.float32), sin.astype(np.float32)


def constants():
    c1 = np.zeros((P, C1_W), np.float32)
    c2 = np.zeros((P, C2_W), np.float32)

    def put(name, value):
        dst, where = (c1, C1) if name in C1 else (c2, C2)
        a, b = where[name]
        dst[:, a:b] = value

    put("ident", np.eye(P))
    put("half", -0.5)
    e, j = np.meshgrid(np.arange(E), np.arange(E), indexing="ij")
    tiny = np.finfo(np.float32).tiny
    put("thr", np.where(j < e, 0.0, np.where(j > e, tiny, 2.0)).reshape(1, E * E))
    cos, sin = rope_tables(np.tile(np.arange(S_CTX), NB), 1.0)
    put("cosk", cos)
    put("sink", sin)
    cos, sin = rope_tables(np.concatenate([positions(t)[0:ATT_ROWS[t]] for t in range(3)]), DH ** -0.5)
    put("cosq", cos)
    put("sinq", sin)
    rows = np.arange(P)
    put("m16", (rows // DH)[:, None] == np.arange(H)[None, :])
    valid = np.zeros(P)
    valid[0:64] = positions(2)[0:64] - WINDOW < S_CTX
    put("valid", valid[:, None])
    put("m8", (rows // NK2)[:, None] == np.arange(H2)[None, :])

    def mask(pos, keys):
        return np.where((keys[None, :] <= pos[:, None]) & (keys[None, :] >= pos[:, None] - WINDOW), 0.0, MASKED)

    cbf = np.zeros((P, CB_W), np.float32)
    cbf[:, 0:P] = np.eye(P)
    cbf[:, P:P + S_CTX] = mask(positions(0), np.arange(S_CTX))
    cbf[:, P + S_CTX:] = mask(positions(2), np.arange(KEY2, S_CTX))
    feature = np.arange(NEXP * P).reshape(NEXP, P)
    sel = (np.tile(np.arange(E), 2)[:, None, None] == feature[None] // F).astype(np.float32)
    return c1, c2, cbf, sel


def kernel(**inputs):
    import ml_dtypes
    import concourse.bacc as bacc
    from concourse.bass_utils import run_bass_kernel_spmd

    a = {n: np.asarray(v) for n, v in inputs.items()}
    x = a["x"]
    xt = np.stack([np.concatenate([x[b, p:p + n] for b, p, n in runs]) for runs in TILES], axis=1)
    swap = np.arange(D).reshape(H, 2, DH // 2)[:, ::-1].reshape(D)
    ctx2 = np.repeat(a["ctx_1024"][:, None, KEY2:, :], H2, axis=1)
    att = {
        "ctxT": a["ctx_1024"].reshape(NB * S_CTX, D).T,
        "ctx2T": ctx2.reshape(NB * R2, D).T,
        "kw": a["L0_xattn_k_w"].T, "kws": a["L0_xattn_k_w"][swap].T, "vw": a["L0_xattn_v_w"].T,
        "qw": a["L0_xattn_q_w"].T, "qws": a["L0_xattn_q_w"][swap].T, "ow": a["L0_xattn_o_w"].T,
        "bias": np.stack([a["L0_xattn_q_b"], a["L0_xattn_q_b"][swap], a["L0_xattn_k_b"], a["L0_xattn_k_b"][swap]], axis=1),
        "gw": a["L0_ffn_gate_w"].T,
    }
    attw = np.concatenate([att[n] for n in AW], axis=1)

    def features(experts, shared):
        flat = np.concatenate([shared, np.zeros((D, NCH * P - HID), np.float32), experts.transpose(1, 0, 2).reshape(D, E * F)], axis=1)
        return flat.reshape(D, NCH, P)

    down = np.concatenate([a["L0_ffn_sw_down"], np.zeros((NCH * P - HID, D), np.float32),
                           a["L0_ffn_w_down"].reshape(E * F, D)])
    wall = np.concatenate([features(a["L0_ffn_w_gate"], a["L0_ffn_sw_gate"]), features(a["L0_ffn_w_up"], a["L0_ffn_sw_up"]),
                           down.reshape(NCH, P, D).transpose(1, 0, 2)], axis=2)
    rows = np.stack([a["L0_xattn_o_b"], a["L0_xattn_v_b"]])
    c1, c2, cbf, sel = constants()
    arrays = {"x_tiles": xt, "attw": attw, "c1": c1, "c2": c2, "cbf": cbf.astype(ml_dtypes.bfloat16), "sel": sel,
              "rows": rows, "wall": wall}
    arrays = {n: np.ascontiguousarray(v) for n, v in arrays.items()}

    nc = bacc.Bacc("TRN2", target_bir_lowering=False, num_devices=1)
    args = [nc.dram_tensor(n, v.shape, mybir.dt.from_np(v.dtype), kind="ExternalInput").ap() for n, v in arrays.items()]
    args.append(nc.dram_tensor("outT", (D, 2, 4 * P), F32, kind="ExternalOutput").ap())
    build(nc, *args)
    r = run_bass_kernel_spmd(nc, [arrays], core_ids=[0])
    outT = r.results[0]["outT"]
    got = np.empty((NB, S, D), np.float32)
    for g, tiles in enumerate(GROUPS):
        for i, t in enumerate(tiles):
            at = i * P
            for b, p, n in TILES[t]:
                got[b, p:p + n] = outT[:, g, at:at + n].T
                at += n
    return got
```
